# Optimizing a Trainium2 kernel written in Bass

```python
import numpy as np
import jax
import jax.numpy as jnp

def _softmax(x, axis=-1):
    return jax.nn.softmax(x, axis=axis)

def _gelu(x):
    return jax.nn.gelu(x, approximate=True)

def _silu(x):
    return jax.nn.silu(x)

def _sigmoid(x):
    return jax.nn.sigmoid(x)

def _layernorm(x, axis=-1, eps=1e-05):
    m = jnp.mean(x, axis=axis, keepdims=True)
    v = jnp.var(x, axis=axis, keepdims=True)
    return (x - m) / jnp.sqrt(v + eps)

def _scatter_add(tgt, idx, src, axis=0):
    return tgt.at[idx].add(src)

def _segment_sum(src, seg, n):
    return jax.ops.segment_sum(src, seg, n)
kernel_name = 'mk_cond_seq_d1_seqx_r8_cb498d'

def setup_inputs(seed: int=0):
    np.random.seed(seed)
    _w = jnp.asarray

    def _rec_inputs():
        import jax
        import jax.numpy as jnp
        _rk = jax.random.key(seed)
        x = -0.0003929 + 0.9999 * jax.random.normal(jax.random.fold_in(_rk, 1), (128, 32, 128), jnp.float32)
        _lenS = 32 - jax.random.randint(jax.random.fold_in(_rk, 7), (128,), 0, max(1, 32 // 4) + 1, jnp.int32)
        _lenS2 = 32 - jax.random.randint(jax.random.fold_in(_rk, 8), (128,), 0, max(1, 32 // 4) + 1, jnp.int32)
        cond_1024 = 0.00782532 + 1.00527 * jax.random.normal(jax.random.fold_in(_rk, 11), (128, 128), jnp.float32)
        return (x, cond_1024)
    x, cond_1024 = _rec_inputs()

    def _L0_cond_setup():
        import jax, jax.numpy as jnp
        import numpy as np
        B, L, D, P = (8, 256, 128, 32)

        def _ln(x):
            m = x.mean(-1, keepdims=True)
            v = x.var(-1, keepdims=True)
            return (x - m) * jax.lax.rsqrt(v + 1e-05)

        def _s5(u, Lam_re, Lam_im, B_re, B_im, C_re, C_im, D_diag, log_step):
            Lam = Lam_re + 1j * Lam_im
            dt = jnp.exp(log_step)
            Lam_bar = jnp.exp(Lam * dt)
            Bc = B_re + 1j * B_im
            B_bar = ((Lam_bar - 1.0) / Lam)[:, None] * Bc
            Bu = jnp.einsum('bld,pd->blp', u.astype(B_bar.dtype), B_bar)
            A = jnp.broadcast_to(Lam_bar, Bu.shape)

            def binop(e1, e2):
                a1, b1 = e1
                a2, b2 = e2
                return (a1 * a2, a2 * b1 + b2)
            _, xs = jax.lax.associative_scan(binop, (A, Bu), axis=1)
            Cc = C_re + 1j * C_im
            return 2.0 * jnp.einsum('blp,dp->bld', xs, Cc).real + D_diag * u
        key = jax.random.key(seed)
        ks = jax.random.split(key, 16)
        inp = {'y': jax.random.normal(ks[0], (B, L, D), jnp.float32), 't': jax.random.normal(ks[1], (B, D), jnp.float32), 'Wm': jax.random.normal(ks[2], (D, 6 * D), jnp.float32) * 0.02, 'bm': jax.random.normal(ks[3], (6 * D,), jnp.float32) * 0.02, 'Lam_re': -0.5 * jnp.ones((P,), jnp.float32), 'Lam_im': jnp.pi * jnp.arange(P, dtype=jnp.float32), 'B_re': jax.random.normal(ks[4], (P, D), jnp.float32) / np.sqrt(D), 'B_im': jax.random.normal(ks[5], (P, D), jnp.float32) / np.sqrt(D), 'C_re': jax.random.normal(ks[6], (D, P), jnp.float32) / np.sqrt(P), 'C_im': jax.random.normal(ks[7], (D, P), jnp.float32) / np.sqrt(P), 'D_diag': jax.random.normal(ks[8], (D,), jnp.float32), 'log_step': jax.random.uniform(ks[9], (P,), jnp.float32, np.log(0.001), np.log(0.1)), 'Wc': jax.random.normal(ks[10], (D, 2 * D), jnp.float32) * 0.02, 'bc': jax.random.normal(ks[11], (2 * D,), jnp.float32) * 0.02, 'W1': jax.random.normal(ks[12], (D, 4 * D), jnp.float32) / np.sqrt(D), 'b1': jnp.zeros((4 * D,), jnp.float32), 'W2': jax.random.normal(ks[13], (4 * D, D), jnp.float32) / np.sqrt(4 * D) * 0.1, 'b2': jnp.zeros((D,), jnp.float32)}
        return inp
    _L0_cond_all = _L0_cond_setup()
    _L0_cond_in = {k: v for k, v in _L0_cond_all.items() if k in ('Wm', 'bm', 'Lam_re', 'Lam_im', 'B_re', 'B_im', 'C_re', 'C_im', 'D_diag', 'log_step', 'Wc', 'bc', 'W1', 'b1', 'W2', 'b2')}
    del _L0_cond_all
    return {'x': x, 'cond_1024': cond_1024, 'L0_cond_Wm': _L0_cond_in['Wm'], 'L0_cond_bm': _L0_cond_in['bm'], 'L0_cond_Lam_re': _L0_cond_in['Lam_re'], 'L0_cond_Lam_im': _L0_cond_in['Lam_im'], 'L0_cond_B_re': _L0_cond_in['B_re'], 'L0_cond_B_im': _L0_cond_in['B_im'], 'L0_cond_C_re': _L0_cond_in['C_re'], 'L0_cond_C_im': _L0_cond_in['C_im'], 'L0_cond_D_diag': _L0_cond_in['D_diag'], 'L0_cond_log_step': _L0_cond_in['log_step'], 'L0_cond_Wc': _L0_cond_in['Wc'], 'L0_cond_bc': _L0_cond_in['bc'], 'L0_cond_W1': _L0_cond_in['W1'], 'L0_cond_b1': _L0_cond_in['b1'], 'L0_cond_W2': _L0_cond_in['W2'], 'L0_cond_b2': _L0_cond_in['b2']}

def reference(x, cond_1024, L0_cond_Wm, L0_cond_bm, L0_cond_Lam_re, L0_cond_Lam_im, L0_cond_B_re, L0_cond_B_im, L0_cond_C_re, L0_cond_C_im, L0_cond_D_diag, L0_cond_log_step, L0_cond_Wc, L0_cond_bc, L0_cond_W1, L0_cond_b1, L0_cond_W2, L0_cond_b2):
    import jax
    import jax.numpy as jnp

    def _L0_cond_ref(y, t, Wm, bm, Lam_re, Lam_im, B_re, B_im, C_re, C_im, D_diag, log_step, Wc, bc, W1, b1, W2, b2):
        import jax, jax.numpy as jnp
        import numpy as np
        B, L, D, P = (8, 256, 128, 32)

        def _ln(x):
            m = x.mean(-1, keepdims=True)
            v = x.var(-1, keepdims=True)
            return (x - m) * jax.lax.rsqrt(v + 1e-05)

        def _s5(u, Lam_re, Lam_im, B_re, B_im, C_re, C_im, D_diag, log_step):
            Lam = Lam_re + 1j * Lam_im
            dt = jnp.exp(log_step)
            Lam_bar = jnp.exp(Lam * dt)
            Bc = B_re + 1j * B_im
            B_bar = ((Lam_bar - 1.0) / Lam)[:, None] * Bc
            Bu = jnp.einsum('bld,pd->blp', u.astype(B_bar.dtype), B_bar)
            A = jnp.broadcast_to(Lam_bar, Bu.shape)

            def binop(e1, e2):
                a1, b1 = e1
                a2, b2 = e2
                return (a1 * a2, a2 * b1 + b2)
            _, xs = jax.lax.associative_scan(binop, (A, Bu), axis=1)
            Cc = C_re + 1j * C_im
            return 2.0 * jnp.einsum('blp,dp->bld', xs, Cc).real + D_diag * u
        mod = t @ Wm + bm
        shift_a, scale_a, gate_a, shift_ff, scale_ff, gate_ff = jnp.split(mod, 6, axis=-1)
        y_mod = _ln(y) * (1 + scale_a[:, None]) + shift_a[:, None]
        a_y = _s5(y_mod, Lam_re, Lam_im, B_re, B_im, C_re, C_im, D_diag, log_step)
        y = y + gate_a[:, None] * a_y
        cond = t @ Wc + bc
        scale_c, shift_c = jnp.split(cond, 2, axis=-1)
        y_norm = _ln(y) * (1 + scale_c[:, None]) + shift_c[:, None]
        y_mod = y_norm * (1 + scale_ff[:, None]) + shift_ff[:, None]
        h = jax.nn.gelu(y_mod @ W1 + b1)
        ff_y = h @ W2 + b2
        return y + gate_ff[:, None] * ff_y
    x = _L0_cond_ref(x, cond_1024, L0_cond_Wm, L0_cond_bm, L0_cond_Lam_re, L0_cond_Lam_im, L0_cond_B_re, L0_cond_B_im, L0_cond_C_re, L0_cond_C_im, L0_cond_D_diag, L0_cond_log_step, L0_cond_Wc, L0_cond_bc, L0_cond_W1, L0_cond_b1, L0_cond_W2, L0_cond_b2)
    return x

_drawn_inputs = setup_inputs


def setup_inputs(seed=0):
    import zlib

    import numpy as np

    out = dict(_drawn_inputs(seed))
    spreads = {'L0_cond_Lam_re': (-0.5, 0.6), 'L0_cond_b1': (0.0, 0.8), 'L0_cond_b2': (0.0, 0.353)}
    factors = {'L0_cond_Wc': 8.0, 'L0_cond_bc': 8.0, 'L0_cond_W1': 3.86, 'L0_cond_W2': 3.385}
    for name, (base, spread) in spreads.items():
        noise = np.random.default_rng([zlib.crc32(name.encode()), seed]).standard_normal(out[name].shape)
        drawn = base * np.exp(spread * noise) if base else spread * noise
        out[name] = jnp.asarray(drawn.astype(out[name].dtype))
    for name, factor in factors.items():
        out[name] = (out[name] * factor).astype(out[name].dtype)
    return out
```

```python
from contextlib import ExitStack

import numpy as np

import concourse.bass as bass
from concourse import mybir

ALU = mybir.AluOpType
ACT = mybir.ActivationFunctionType
F32 = mybir.dt.float32
F32R = mybir.dt.float32r
I32 = mybir.dt.int32

STEPS = 4
PSUM_COLUMNS = 512

SERIES = [1.0, 1 / 2, 1 / 6, 1 / 24, 1 / 120, 1 / 720, 1 / 5040, 1 / 40320]
ROUND = 1.5 * 2.0 ** 23
LOG2E = float(np.log2(np.e))
LN2_HI = 0.693359375
LN2_LO = float(np.log(2.0) - LN2_HI)
TWO_PI_HI = 6.28125
TWO_PI_MID = float(np.float32(2 * np.pi - TWO_PI_HI))
TWO_PI_LO = float(2 * np.pi - TWO_PI_HI - TWO_PI_MID)
PI_BELOW = 3.1415925
LN_EPS = 1e-5


def conditioned_s5_block(nc, x, cond, Wm, bm, Lam_re, Lam_im, B_re, B_im, C_re, C_im, D_diag,
                         log_step, Wc, bc, W1, b1, W2, b2, out):
    NB, L, D = x.shape
    P = Lam_re.shape[0]
    FF = W1.shape[1]
    NC = L // STEPS
    NF = FF // D
    CW = STEPS * D
    HB = NB // 2
    R = 2 * P
    assert NB == D == 128 and P == 32 and CW == PSUM_COLUMNS and NF * D == FF

    with ExitStack() as ctx:
        def sb(name, shape, dt=F32):
            return ctx.enter_context(nc.sbuf_tensor(name, shape, dt))

        def bank(name):
            return ctx.enter_context(nc.psum_tensor(name, [128, PSUM_COLUMNS], F32))

        def sem(name):
            return ctx.enter_context(nc.semaphore(name))

        cond_sb = sb("cond_sb", [NB, D])
        condT = sb("condT", [D, NB])
        wmod = sb("wmod", [D, 8 * D])
        mod_bias = sb("mod_bias", [1, 8 * D])
        free_rows = sb("free_rows", [1, 2 * D])
        ones_row = sb("ones_row", [1, 128])
        ident = sb("ident", [128, 128])
        same_half = sb("same_half", [128, R])
        swap_parts = sb("swap_parts", [128, R])
        b1_rows = sb("b1_rows", [NF, D])
        b1_col = sb("b1_col", [D, NF])
        w1_sb = sb("w1_sb", [D, FF])
        w1_hi = sb("w1_hi", [D, FF], F32R)
        w1_lo = sb("w1_lo", [D, FF], F32R)
        w2_sb = sb("w2_sb", [D, NF, D])
        scale1 = sb("scale1", [D, NB])
        shift1 = sb("shift1", [D, NB])
        scale_ff = sb("scale_ff", [D, NB])
        scale2 = sb("scale2", [D, NB])
        shift2a = sb("shift2a", [D, NB])
        shift2 = sb("shift2", [D, NB])
        gate_a = sb("gate_a", [NB, D])
        gate_d = sb("gate_d", [NB, D])
        gate_ds = sb("gate_ds", [NB, D])
        gate_dh = sb("gate_dh", [NB, D])
        gate_ff = sb("gate_ff", [NB, D])
        gate_b2 = sb("gate_b2", [NB, D])

        lam = sb("lam", [128, 3])
        series_even = sb("series_even", [128, 4])
        series_odd = sb("series_odd", [128, 4])
        step_no = sb("step_no", [128, STEPS + 1])
        sign = sb("sign", [128, 1])
        col = sb("col", [128, 128])
        phi = sb("phi", [128, 5, STEPS + 1])
        angles = sb("angles", [128, 2, STEPS + 1])
        sines = sb("sines", [128, 2, STEPS + 1])
        b_ab = sb("b_ab", [R, 2, D])
        b_part = sb("b_part", [R, STEPS, D])
        b_turned = sb("b_turned", [R, STEPS, D])
        bT = sb("bT", [D, STEPS, R])
        c_parts = sb("c_parts", [D, 5, P])
        cT = sb("cT", [128, 2, D])
        c_part = sb("c_part", [128, STEPS, D])
        c_turned = sb("c_turned", [128, STEPS, D])
        next_frame_part = sb("next_frame_part", [128, R])
        next_frame = sb("next_frame", [128, R])

        x_sb = sb("x_sb", [NB, NC, CW])
        n1 = sb("n1", [NB, NC, CW])
        u_part = sb("u_part", [D, 2, CW])
        uT = sb("uT", [D, 2, CW])
        z = sb("z", [128, NC, STEPS, HB])
        skip_a = sb("skip_a", [NB, 2, CW])
        skip_b = sb("skip_b", [NB, 2, CW])
        skip = sb("skip", [NB, 2, CW])
        gated = sb("gated", [NB, 2, CW])
        y1 = sb("y1", [NB, NC, CW])
        y1b = sb("y1b", [NB, NC, CW])
        n2 = sb("n2", [NB, 2, CW])
        v_part = sb("v_part", [D, 2, CW])
        v = sb("v", [D, 2, CW])
        v_hi = sb("v_hi", [D, 2, CW], F32R)
        v_lo = sb("v_lo", [D, 2, CW], F32R)
        h = sb("h", [D, 2, NF, CW])
        gated_ff = sb("gated_ff", [NB, 2, CW])
        y2 = sb("y2", [NB, NC, CW])
        raw_stats = [sb(f"raw_stats{k}", [NB, NC, STEPS, 6]) for k in (1, 2)]
        mean_var = [sb(f"mean_var{k}", [NB, NC, STEPS, 2]) for k in (1, 2)]
        var_eps = [sb(f"var_eps{k}", [NB, NC, STEPS]) for k in (1, 2)]
        neg_mean = [sb(f"neg_mean{k}", [NB, NC, STEPS]) for k in (1, 2)]
        rstd = [sb(f"rstd{k}", [NB, NC, STEPS]) for k in (1, 2)]
        norm_bias = [sb(f"norm_bias{k}", [NB, NC, STEPS]) for k in (1, 2)]
        minus_half = sb("minus_half", [NB, STEPS])

        p_t1, p_t2, p_b, p_c = bank("p_t1"), bank("p_t2"), bank("p_b"), bank("p_c")
        p_h = [bank("p_h0"), bank("p_h1")]
        p_y = [bank("p_y0"), bank("p_y1")]

        x_landed = [sem(f"x_landed{c}") for c in range(NC)]
        lam_landed, b_landed, c_landed = sem("lam_landed"), sem("b_landed"), sem("c_landed")
        cond_landed, wmod_landed = sem("cond_landed"), sem("wmod_landed")
        rows_landed = sem("rows_landed")
        w1_landed, w2_landed, b1_landed = sem("w1_landed"), sem("w2_landed"), sem("b1_landed")
        const_chain, ident_ready, const_ready = sem("const_chain"), sem("ident_ready"), sem("const_ready")
        chain = sem("chain")
        angles_ready, sines_ready = sem("angles_ready"), sem("sines_ready")
        b_turned_ready, bT_in_psum, bT_ready = sem("b_turned_ready"), sem("bT_in_psum"), sem("bT_ready")
        cT_in_psum, cT_ready = sem("cT_in_psum"), sem("cT_ready")
        c_turned_ready = sem("c_turned_ready")
        condT_in_psum, condT_ready = sem("condT_in_psum"), sem("condT_ready")
        mod1_in_psum, mod2_in_psum = sem("mod1_in_psum"), sem("mod2_in_psum")
        gates_in_psum = sem("gates_in_psum")
        scale1_ready, mod2_read, gates_ready = sem("scale1_ready"), sem("mod2_read"), sem("gates_ready")
        scale2_ready = sem("scale2_ready")
        w1_split = sem("w1_split")
        ones_ready, next_frame_ready, b1_col_ready = sem("ones_ready"), sem("next_frame_ready"), sem("b1_col_ready")
        stats_ready = [sem("stats1_ready"), sem("stats2_ready")]
        rstd_ready = [sem("rstd1_ready"), sem("rstd2_ready")]
        rstd_chain = sem("rstd_chain")
        n_ready = [sem("n1_ready"), sem("n2_ready")]
        n1T_in_psum, n2T_in_psum = sem("n1T_in_psum"), sem("n2T_in_psum")
        u_part_ready, uT_ready = sem("u_part_ready"), sem("uT_ready")
        b_done, z_ready = sem("b_done"), sem("z_ready")
        c_done = sem("c_done")
        skip_chain, skip_ready = sem("skip_chain"), sem("skip_ready")
        gated_ready, y1_ready, y1b_ready = sem("gated_ready"), sem("y1_ready"), sem("y1b_ready")
        raw_ready, mv_ready = sem("raw_ready"), sem("mv_ready")
        v_part_ready, v_ready = sem("v_part_ready"), sem("v_ready")
        v_hi_ready, v_lo_ready = sem("v_hi_ready"), sem("v_lo_ready")
        w1_done, h_ready, w2_done = sem("w1_done"), sem("h_ready"), sem("w2_done")
        gated_ff_ready, y2_ready, stored = sem("gated_ff_ready"), sem("y2_ready"), sem("stored")

        def over_steps(table):
            return table[:, :].unsqueeze(1).to_broadcast([128, STEPS, 128])

        def steps(ap):
            return ap.rearrange("p (s d) -> p s d", s=STEPS)

        block = ctx.enter_context(nc.Block())

        @block.sync
        def _(sp):
            def load_x(c):
                sp.dma_start(x_sb[:, c, :], x[:, c * STEPS:(c + 1) * STEPS, :].rearrange("b s d -> b (s d)")) \
                  .then_inc(x_landed[c], 16)

            load_x(0)
            sp.dma_start(cond_sb[:, :], cond).then_inc(cond_landed, 16)
            sp.dma_start(wmod[:, 0:6 * D], Wm).then_inc(wmod_landed, 16)
            sp.dma_start(wmod[:, 6 * D:8 * D], Wc).then_inc(wmod_landed, 16)
            load_x(1)
            load_x(2)
            sp.dma_start(w1_sb[:, :], W1).then_inc(w1_landed, 16)
            sp.dma_start(w2_sb[:, :, :], W2.rearrange("(f k) d -> k f d", k=D)).then_inc(w2_landed, 16)
            for c in range(3, NC):
                load_x(c)
            for c in range(NC):
                sp.wait_ge(y2_ready, c + 1)
                sp.dma_start(out[:, c * STEPS:(c + 1) * STEPS, :].rearrange("b s d -> b (s d)"), y2[:, c, :]) \
                  .then_inc(stored, 16)
            sp.wait_ge(stored, 16 * NC)

        @block.gpsimd
        def _(pool):
            n = [0]

            def const_link(ins):
                n[0] += 1
                ins.then_inc(const_chain, 1)
                pool.wait_ge(const_chain, n[0])

            pool.dma_start(mod_bias[:, 0:6 * D], bm.rearrange("(o n) -> o n", o=1)).then_inc(rows_landed, 16)
            pool.dma_start(mod_bias[:, 6 * D:8 * D], bc.rearrange("(o n) -> o n", o=1)).then_inc(rows_landed, 16)
            pool.dma_start(free_rows[:, 0:D], D_diag.rearrange("(o n) -> o n", o=1)).then_inc(rows_landed, 16)
            pool.dma_start(free_rows[:, D:2 * D], b2.rearrange("(o n) -> o n", o=1)).then_inc(rows_landed, 16)
            pool.dma_start(b1_rows[:, :], b1.rearrange("(f d) -> f d", f=NF)).then_inc(b1_landed, 16)

            def mark(table, offsets):
                for at in offsets:
                    ins = pool.affine_select(out=table[:, :], in_=table[:, :], compare_op=ALU.not_equal, fill=1.0,
                                             base=-at, pattern=[[-1, table.shape[1]]], channel_multiplier=1)
                    if at != offsets[-1]:
                        const_link(ins)
                return ins

            const_link(pool.memset(ident[:, :], 0.0))
            mark(ident, [0]).then_inc(ident_ready, 1)
            pool.memset(minus_half[:, :], -0.5)
            pool.memset(same_half[:, :], 0.0)
            const_link(pool.memset(swap_parts[:, :], 0.0))
            mark(same_half, [0, R]).then_inc(const_ready, 1)
            mark(swap_parts, [-P, P, 3 * P]).then_inc(const_ready, 1)

            def rstd_of(k, c):
                pool.wait_ge(stats_ready[k], c + 1)
                pool.tensor_tensor(rstd[k][:, c, :], var_eps[k][:, c, :], minus_half[:, :], ALU.pow) \
                    .then_inc(rstd_chain, 1)
                n[1] += 1
                pool.wait_ge(rstd_chain, n[1])
                pool.tensor_tensor(norm_bias[k][:, c, :], neg_mean[k][:, c, :], rstd[k][:, c, :], ALU.mult) \
                    .then_inc(rstd_ready[k], 1)

            def skip_path(c):
                s = c % 2
                if c == 0:
                    pool.wait_ge(gates_ready, 1)
                pool.wait_ge(n_ready[0], c + 1)
                pool.tensor_tensor(steps(skip_a[:, s, :]), steps(n1[:, c, :]), over_steps(gate_ds), ALU.mult) \
                    .then_inc(skip_chain, 1)
                pool.wait_ge(skip_chain, 2 * c + 1)
                pool.tensor_tensor(steps(skip_b[:, s, :]), steps(skip_a[:, s, :]), over_steps(gate_dh), ALU.add) \
                    .then_inc(skip_chain, 1)
                if c >= 2:
                    pool.wait_ge(y1_ready, c - 1)
                pool.wait_ge(skip_chain, 2 * c + 2)
                pool.tensor_tensor(skip[:, s, :], skip_b[:, s, :], x_sb[:, c, :], ALU.add).then_inc(skip_ready, 1)

            def add_ff_bias(c):
                pool.wait_ge(y1_ready, c + 1)
                pool.tensor_tensor(steps(y1b[:, c, :]), steps(y1[:, c, :]), over_steps(gate_b2), ALU.add) \
                    .then_inc(y1b_ready, 1)

            n.append(0)
            for i in range(-3, NC):
                if 0 <= i + 1 < NC:
                    rstd_of(1, i + 1)
                    add_ff_bias(i + 1)
                if 0 <= i + 3 < NC:
                    rstd_of(0, i + 3)
                    skip_path(i + 3)

        @block.vector
        def _(dve):
            count = {"chain": 0, "raw": 0, "mv": 0}

            def link(ins):
                count["chain"] += 1
                ins.then_inc(chain, 1)
                dve.wait_ge(chain, count["chain"])

            def note(ins):
                count["chain"] += 1
                ins.then_inc(chain, 1)

            def noted():
                dve.wait_ge(chain, count["chain"])

            cells = iter(range(128))

            def cell(width=1):
                at = [next(cells) for _ in range(width)]
                return col[:, at[0]:at[-1] + 1]

            def stats(k, c):
                if k == 0:
                    src = x_sb
                    dve.wait_ge(x_landed[c], 16)
                else:
                    src = y1
                    dve.wait_ge(y1_ready, c + 1)
                for j in range(STEPS):
                    ins = dve.bn_stats(raw_stats[k][:, c, j, :], src[:, c, j * D:(j + 1) * D])
                ins.then_inc(raw_ready, 1)
                count["raw"] += 1
                dve.wait_ge(raw_ready, count["raw"])
                for j in range(STEPS):
                    ins = dve.bn_aggr(mean_var[k][:, c, j, :], raw_stats[k][:, c, j, :])
                ins.then_inc(mv_ready, 1)
                count["mv"] += 1
                dve.wait_ge(mv_ready, count["mv"])
                dve.tensor_scalar(var_eps[k][:, c, :], mean_var[k][:, c, :, 1], LN_EPS, None, ALU.add)
                dve.tensor_scalar(neg_mean[k][:, c, :], mean_var[k][:, c, :, 0], -1.0, None, ALU.mult) \
                   .then_inc(stats_ready[k], 1)

            def exp_parts(arg):
                clamped, shifted, whole, f1, f = cell(), cell(), cell(), cell(), cell()
                link(dve.tensor_scalar(clamped, arg, -87.0, 88.0, ALU.max, ALU.min))
                link(dve.tensor_scalar(shifted, clamped, LOG2E, ROUND, ALU.mult, ALU.add))
                link(dve.tensor_scalar(whole, shifted, ROUND, None, ALU.subtract))
                link(dve.scalar_tensor_tensor(f1, whole, -LN2_HI, clamped, ALU.mult, ALU.add))
                link(dve.scalar_tensor_tensor(f, whole, -LN2_LO, f1, ALU.mult, ALU.add))
                power_bits = cell().bitcast(I32)
                note(dve.tensor_scalar(power_bits, whole, 127.0, 2.0 ** 23, ALU.add, ALU.mult))
                f2, f4, s4, s2, s1, m1 = cell(), cell(), cell(4), cell(2), cell(), cell()
                note(dve.tensor_tensor(f2, f, f, ALU.mult))
                link(dve.scalar_tensor_tensor(s4, series_odd[:, :], f, series_even[:, :], ALU.mult, ALU.add))
                note(dve.tensor_tensor(f4, f2, f2, ALU.mult))
                link(dve.scalar_tensor_tensor(s2, s4[:, 1::2], f2, s4[:, 0::2], ALU.mult, ALU.add))
                link(dve.scalar_tensor_tensor(s1, s2[:, 1:2], f4, s2[:, 0:1], ALU.mult, ALU.add))
                link(dve.tensor_tensor(m1, s1, f, ALU.mult))
                return power_bits.bitcast(F32), m1

            for k in range(4):
                dve.memset(series_even[:, k:k + 1], SERIES[2 * k])
                dve.memset(series_odd[:, k:k + 1], SERIES[2 * k + 1])
            for j in range(STEPS + 1):
                dve.memset(step_no[:, j:j + 1], float(j))
            note(dve.memset(sign[:, :], 1.0))
            dve.memset(ones_row[:, :], 1.0).then_inc(ones_ready, 1)
            noted()
            dve.memset(sign[0:P, :], -1.0)
            note(dve.memset(sign[2 * P:3 * P, :], -1.0))

            dve.wait_ge(lam_landed, 48)
            power, m1 = exp_parts(lam[:, 2:3])
            dt = cell()
            link(dve.scalar_tensor_tensor(dt, m1, power, power, ALU.mult, ALU.add))
            theta, decay_log = cell(), cell()
            note(dve.tensor_tensor(theta, lam[:, 1:2], dt, ALU.mult))
            link(dve.tensor_tensor(decay_log, lam[:, 0:1], dt, ALU.mult))

            W = STEPS + 1
            angle, turns_s, turns, a1, a2 = (phi[:, k, :] for k in range(5))
            link(dve.tensor_scalar(angle, step_no[:, :], theta, None, ALU.mult))
            link(dve.tensor_scalar(turns_s, angle, float(1 / (2 * np.pi)), ROUND, ALU.mult, ALU.add))
            link(dve.tensor_scalar(turns, turns_s, ROUND, None, ALU.subtract))
            link(dve.scalar_tensor_tensor(a1, turns, -TWO_PI_HI, angle, ALU.mult, ALU.add))
            link(dve.scalar_tensor_tensor(a2, turns, -TWO_PI_MID, a1, ALU.mult, ALU.add))
            a3 = cell(W)
            link(dve.scalar_tensor_tensor(a3, turns, -TWO_PI_LO, a2, ALU.mult, ALU.add))
            note(dve.tensor_scalar(angles[:, 0, :], a3, -PI_BELOW, PI_BELOW, ALU.max, ALU.min))
            dve.tensor_scalar(angles[:, 1, :], a3, 0.5, None, ALU.mult).then_inc(angles_ready, 1)

            power, m1 = exp_parts(decay_log)
            power_m1, decay_m1, decay = cell(), cell(), cell()
            note(dve.scalar_tensor_tensor(decay, m1, power, power, ALU.mult, ALU.add))
            link(dve.tensor_scalar(power_m1, power, -1.0, None, ALU.add))
            link(dve.scalar_tensor_tensor(decay_m1, m1, power, power_m1, ALU.mult, ALU.add))
            sq_im, norm2, inv_norm2 = cell(), cell(), cell()
            link(dve.tensor_tensor(sq_im, lam[:, 1:2], lam[:, 1:2], ALU.mult))
            link(dve.scalar_tensor_tensor(norm2, lam[:, 0:1], lam[:, 0:1], sq_im, ALU.mult, ALU.add))
            link(dve.reciprocal(inv_norm2, norm2))

            stats(0, 0)

            sin = sines[:, 0, :]
            half_sq, cos = cell(W), cell(W)
            dve.wait_ge(sines_ready, 1)
            link(dve.tensor_tensor(half_sq, sines[:, 1, :], sines[:, 1, :], ALU.mult))
            cos_m1, num_re, num_im, t1, t2, t3, t4 = (cell() for _ in range(7))
            q_re, q_im, neg_q_re, w_re_a, w_im_a = cell(), cell(), cell(), cell(W), cell(W)
            w_re, w_im = cell(W), cell(W)
            note(dve.tensor_scalar(cos, half_sq, -2.0, 1.0, ALU.mult, ALU.add))
            note(dve.tensor_scalar(cos_m1, half_sq[:, 1:2], -2.0, None, ALU.mult))
            link(dve.tensor_tensor(num_im, decay, sin[:, 1:2], ALU.mult))
            note(dve.scalar_tensor_tensor(num_re, decay_m1, cos[:, 1:2], cos_m1, ALU.mult, ALU.add))
            note(dve.tensor_tensor(t1, num_im, lam[:, 1:2], ALU.mult))
            link(dve.tensor_tensor(t2, num_im, lam[:, 0:1], ALU.mult))
            note(dve.scalar_tensor_tensor(t3, num_re, lam[:, 0:1], t1, ALU.mult, ALU.add))
            link(dve.scalar_tensor_tensor(t4, num_re, lam[:, 1:2], t2, ALU.mult, ALU.subtract))
            note(dve.tensor_tensor(q_re, t3, inv_norm2, ALU.mult))
            link(dve.scalar_tensor_tensor(q_im, t4, -1.0, inv_norm2, ALU.mult, ALU.mult))
            note(dve.tensor_scalar(w_re_a, cos, q_re, None, ALU.mult))
            link(dve.tensor_scalar(w_im_a, sin, q_re, None, ALU.mult))
            note(dve.scalar_tensor_tensor(w_re, sin, q_im, w_re_a, ALU.mult, ALU.add))
            w_im_b = cell(W)
            link(dve.scalar_tensor_tensor(w_im_b, cos, q_im, w_im_a, ALU.mult, ALU.subtract))
            link(dve.tensor_scalar(w_im, w_im_b, sign[:, 0:1], None, ALU.mult))
            dve.wait_ge(b_landed, 64)
            for j in range(STEPS):
                note(dve.tensor_scalar(b_part[:, j, :], b_ab[:, 1, :], w_im[0:R, j:j + 1], None, ALU.mult))
            noted()
            for j in range(STEPS):
                ins = dve.scalar_tensor_tensor(b_turned[:, j, :], b_ab[:, 0, :], w_re[0:R, j:j + 1], b_part[:, j, :],
                                               ALU.mult, ALU.add)
            ins.then_inc(b_turned_ready, 1)

            dve.wait_ge(mod1_in_psum, 1)
            note(dve.tensor_scalar(scale1[:, :], p_h[0][:, 0:128], 1.0, None, ALU.add))
            dve.tensor_copy(shift1[:, :], p_h[0][:, 128:256]).then_inc(scale1_ready, 1)
            noted()

            dve.wait_ge(bT_in_psum, 1)
            dve.tensor_copy(bT[:, :, :], p_t2[:, 0:STEPS * R].rearrange("p (s r) -> p s r", s=STEPS)) \
               .then_inc(bT_ready, 1)

            f_re, f_im, f_im_s = cell(), cell(), cell()
            note(dve.tensor_tensor(f_re, decay, cos[:, STEPS:W], ALU.mult))
            link(dve.tensor_tensor(f_im, decay, sin[:, STEPS:W], ALU.mult))
            link(dve.scalar_tensor_tensor(f_im_s, f_im, -1.0, sign[:, :], ALU.mult, ALU.mult))
            dve.wait_ge(const_ready, 2)
            link(dve.tensor_scalar(next_frame_part[:, :], same_half[:, :], f_re, None, ALU.mult))
            dve.scalar_tensor_tensor(next_frame[:, :], swap_parts[:, :], f_im_s, next_frame_part[:, :],
                                     ALU.mult, ALU.add).then_inc(next_frame_ready, 1)
            c_re, c_im = cell(W), cell(W)
            note(dve.tensor_scalar(c_im, sin, -2.0, None, ALU.mult))
            link(dve.tensor_scalar(c_re, cos, sign[:, 0:1], -2.0, ALU.mult, ALU.mult))
            dve.wait_ge(cT_ready, 1)
            for j in range(STEPS):
                note(dve.tensor_scalar(c_part[:, j, :], cT[:, 1, :], c_im[:, j:j + 1], None, ALU.mult))
            noted()
            for j in range(STEPS):
                ins = dve.scalar_tensor_tensor(c_turned[:, j, :], cT[:, 0, :], c_re[:, j:j + 1], c_part[:, j, :],
                                               ALU.mult, ALU.add)
            ins.then_inc(c_turned_ready, 1)

            def second_tables():
                dve.wait_ge(gates_in_psum, 1)
                note(dve.tensor_copy(gate_a[:, :], p_y[0][:, 2 * D:3 * D]))
                note(dve.tensor_copy(gate_ff[:, :], p_y[0][:, 3 * D:4 * D]))
                noted()
                note(dve.tensor_tensor(gate_d[:, :], gate_a[:, :], p_c[:, 0:D], ALU.mult))
                note(dve.tensor_tensor(gate_b2[:, :], gate_ff[:, :], p_c[:, D:2 * D], ALU.mult))
                noted()
                note(dve.tensor_tensor(gate_dh[:, :], gate_d[:, :], p_y[0][:, 0:D], ALU.mult))
                dve.scalar_tensor_tensor(gate_ds[:, :], p_y[0][:, D:2 * D], 1.0, gate_d[:, :], ALU.add, ALU.mult) \
                   .then_inc(gates_ready, 1)
                dve.wait_ge(mod2_in_psum, 1)
                link(dve.tensor_scalar(scale_ff[:, :], p_h[1][:, D:2 * D], 1.0, None, ALU.add))
                note(dve.scalar_tensor_tensor(scale2[:, :], p_h[1][:, 2 * D:3 * D], 1.0, scale_ff[:, :],
                                              ALU.add, ALU.mult))
                link(dve.tensor_tensor(shift2a[:, :], p_h[1][:, 3 * D:4 * D], scale_ff[:, :], ALU.mult))
                dve.tensor_tensor(shift2[:, :], p_h[1][:, 0:D], shift2a[:, :], ALU.add).then_inc(scale2_ready, 1)

            def split_w1():
                dve.wait_ge(w1_landed, 16)
                link(dve.tensor_copy(w1_hi[:, :], w1_sb[:, :]))
                dve.tensor_tensor(w1_lo[:, :], w1_sb[:, :], w1_hi[:, :].bitcast(F32), ALU.subtract) \
                   .then_inc(w1_split, 1)

            def modulate_u(c):
                s = c % 2
                dve.wait_ge(n1T_in_psum, c + 1)
                if c == 0:
                    dve.wait_ge(scale1_ready, 1)
                dve.tensor_tensor(steps(u_part[:, s, :]), steps(p_t1[:, :]), over_steps(scale1), ALU.mult) \
                   .then_inc(u_part_ready, 1)
                dve.wait_ge(u_part_ready, c + 1)
                dve.tensor_tensor(steps(uT[:, s, :]), steps(u_part[:, s, :]), over_steps(shift1), ALU.add) \
                   .then_inc(uT_ready, 1)

            def recur(c):
                dve.wait_ge(b_done, c + 1)
                dve.tensor_copy(z[:, c, 0, :], p_b[:, 0:HB]).then_inc(z_ready, 1)
                for j in range(1, STEPS):
                    dve.wait_ge(z_ready, STEPS * c + j)
                    dve.scalar_tensor_tensor(z[:, c, j, :], z[:, c, j - 1, :], decay, p_b[:, j * HB:(j + 1) * HB],
                                             ALU.mult, ALU.add).then_inc(z_ready, 1)

            def add_state_layer(c):
                s = c % 2
                dve.wait_ge(c_done, c + 1)
                dve.tensor_tensor(steps(gated[:, s, :]), steps(p_c[:, :]), over_steps(gate_a), ALU.mult) \
                   .then_inc(gated_ready, 1)
                dve.wait_ge(skip_ready, c + 1)
                dve.wait_ge(gated_ready, c + 1)
                dve.tensor_tensor(y1[:, c, :], gated[:, s, :], skip[:, s, :], ALU.add).then_inc(y1_ready, 1)

            def modulate_v(c):
                s = c % 2
                dve.wait_ge(n2T_in_psum, c + 1)
                dve.tensor_tensor(steps(v_part[:, s, :]), steps(p_t2[:, :]), over_steps(scale2), ALU.mult) \
                   .then_inc(v_part_ready, 1)
                dve.wait_ge(v_part_ready, c + 1)
                if c >= 2:
                    dve.wait_ge(v_hi_ready, c - 1)
                dve.tensor_tensor(steps(v[:, s, :]), steps(v_part[:, s, :]), over_steps(shift2), ALU.add) \
                   .then_inc(v_ready, 1)
                if c >= 2:
                    dve.wait_ge(w1_done, NF * (c - 1))
                dve.wait_ge(v_hi_ready, c + 1)
                dve.tensor_tensor(v_lo[:, s, :], v[:, s, :], v_hi[:, s, :].bitcast(F32), ALU.subtract) \
                   .then_inc(v_lo_ready, 1)

            def add_ff(c):
                s = c % 2
                dve.wait_ge(w2_done, c + 1)
                dve.tensor_tensor(steps(gated_ff[:, s, :]), steps(p_y[s][:, :]), over_steps(gate_ff), ALU.mult) \
                   .then_inc(gated_ff_ready, 1)
                dve.wait_ge(gated_ff_ready, c + 1)
                dve.wait_ge(y1b_ready, c + 1)
                dve.tensor_tensor(y2[:, c, :], gated_ff[:, s, :], y1b[:, c, :], ALU.add).then_inc(y2_ready, 1)

            for i in range(-2, NC + 1):
                if i == -1:
                    second_tables()
                    split_w1()
                if 0 <= i + 1 < NC:
                    add_state_layer(i + 1)
                    stats(1, i + 1)
                if 0 <= i - 1 < NC:
                    add_ff(i - 1)
                if 0 <= i + 2 < NC:
                    modulate_u(i + 2)
                if 0 <= i + 3 < NC:
                    stats(0, i + 3)
                if 0 <= i + 2 < NC:
                    recur(i + 2)
                if 0 <= i + 1 < NC:
                    modulate_v(i + 1)

        @block.scalar
        def _(act):
            def groups_of(source, k):
                act.dma_start(lam[:, k:k + 1], source.rearrange("(g p o) -> g p o", g=1, o=1)
                              .broadcast_to([4, P, 1])).then_inc(lam_landed, 16)

            groups_of(log_step, 2)
            groups_of(Lam_im, 1)
            groups_of(Lam_re, 0)
            act.dma_start(b_ab[0:P, 0, :], B_re).then_inc(b_landed, 16)
            act.dma_start(b_ab[P:R, 0, :], B_im).then_inc(b_landed, 16)
            act.dma_start(b_ab[0:P, 1, :], B_im).then_inc(b_landed, 16)
            act.dma_start(b_ab[P:R, 1, :], B_re).then_inc(b_landed, 16)
            act.dma_start(c_parts[:, 0::2, :], C_re.rearrange("d (o p) -> d o p", o=1).broadcast_to([D, 3, P])) \
               .then_inc(c_landed, 16)
            act.dma_start(c_parts[:, 1::2, :], C_im.rearrange("d (o p) -> d o p", o=1).broadcast_to([D, 2, P])) \
               .then_inc(c_landed, 16)

            act.wait_ge(condT_in_psum, 1)
            nc.scalar.copy(condT[:, :], p_b[:, 0:NB]).then_inc(condT_ready, 1)

            def norm(k, c):
                dst = n1[:, c, :] if k == 0 else n2[:, c % 2, :]
                src = x_sb[:, c, :] if k == 0 else y1[:, c, :]
                act.wait_ge(rstd_ready[k], c + 1)
                if k == 1 and c >= 2:
                    act.wait_ge(n2T_in_psum, c - 1)
                for j in range(STEPS):
                    ins = nc.scalar.activation(dst[:, j * D:(j + 1) * D], src[:, j * D:(j + 1) * D], ACT.Identity,
                                               bias=norm_bias[k][:, c, j:j + 1], scale=rstd[k][:, c, j:j + 1])
                ins.then_inc(n_ready[k], 1)

            def gelu(c):
                s = c % 2
                if c == 0:
                    act.wait_ge(b1_col_ready, 1)
                if c >= 2:
                    act.wait_ge(w2_done, c - 1)
                for f in range(NF):
                    act.wait_ge(w1_done, NF * c + f + 1)
                    nc.scalar.activation(h[:, s, f, :], p_h[f % 2][:, :], ACT.Gelu_apprx_tanh,
                                         bias=b1_col[:, f:f + 1]).then_inc(h_ready, 1)

            def split_v(c):
                s = c % 2
                if c >= 2:
                    act.wait_ge(w1_done, NF * (c - 1))
                act.wait_ge(v_ready, c + 1)
                nc.scalar.copy(v_hi[:, s, :], v[:, s, :]).then_inc(v_hi_ready, 1)

            act.wait_ge(angles_ready, 1)
            nc.scalar.activation(sines[:, :, :], angles[:, :, :], ACT.Sin) \
              .then_inc(sines_ready, 1)
            act.wait_ge(cT_in_psum, 1)
            nc.scalar.copy(cT[:, :, :], p_y[1][:, 0:2 * D].rearrange("p (k d) -> p k d", k=2)).then_inc(cT_ready, 1)
            nc.scalar.copy(b1_col[:, :], p_y[1][:, 2 * D:2 * D + NF]).then_inc(b1_col_ready, 1)

            for i in range(-3, NC):
                if 0 <= i < NC:
                    gelu(i)
                if 0 <= i + 1 < NC:
                    norm(1, i + 1)
                    split_v(i + 1)
                if 0 <= i + 3 < NC:
                    norm(0, i + 3)

        @block.tensor
        def _(pe):
            def turn(dst, src, k):
                return pe.transpose(dst, src, ident[0:k, 0:k])

            pe.wait_ge(ident_ready, 1)
            pe.wait_ge(cond_landed, 16)
            turn(p_b[:, 0:NB], cond_sb[:, :], NB).then_inc(condT_in_psum, 1)
            pe.wait_ge(c_landed, 32)
            turn(p_y[1][:, 0:D], c_parts[:, 0:4, :].rearrange("d g p -> d (g p)"), D)
            turn(p_y[1][:, D:2 * D], c_parts[:, 1:5, :].rearrange("d g p -> d (g p)"), D)
            pe.wait_ge(b1_landed, 16)
            turn(p_y[1][:, 2 * D:2 * D + NF], b1_rows[:, :], NF).then_inc(cT_in_psum, 1)

            def modulation_columns(dst, first):
                pe.matmul(dst, wmod[:, first:first + D], condT[:, :], start=True, stop=False)
                return pe.matmul(dst, mod_bias[:, first:first + D], ones_row[:, :], start=False, stop=True)

            def modulation_rows(dst, first, width):
                pe.matmul(dst, condT[:, :], wmod[:, first:first + width], start=True, stop=False)
                return pe.matmul(dst, ones_row[:, :], mod_bias[:, first:first + width], start=False, stop=True)

            pe.wait_ge(condT_ready, 1)
            pe.wait_ge(wmod_landed, 32)
            pe.wait_ge(rows_landed, 64)
            pe.wait_ge(ones_ready, 1)
            modulation_columns(p_h[0][:, 0:D], D)
            modulation_columns(p_h[0][:, D:2 * D], 0).then_inc(mod1_in_psum, 1)
            modulation_rows(p_y[0][:, 0:3 * D], 0, 3 * D)
            modulation_rows(p_y[0][:, 3 * D:4 * D], 5 * D, D)
            pe.matmul(p_c[:, 0:2 * D], ones_row[:, :], free_rows[:, :], start=True, stop=True) \
              .then_inc(gates_in_psum, 1)
            for k, first in enumerate([3 * D, 4 * D, 6 * D, 7 * D]):
                last = modulation_columns(p_h[1][:, k * D:(k + 1) * D], first)
            last.then_inc(mod2_in_psum, 1)
            pe.wait_ge(b_turned_ready, 1)
            for j in range(STEPS):
                last = turn(p_t2[:, j * R:(j + 1) * R], b_turned[:, j, :], R)
            last.then_inc(bT_in_psum, 1)

            def turn_n1(c):
                pe.wait_ge(n_ready[0], c + 1)
                if c >= 1:
                    pe.wait_ge(u_part_ready, c)
                for j in range(STEPS):
                    last = turn(p_t1[:, j * D:(j + 1) * D], n1[:, c, j * D:(j + 1) * D], NB)
                last.then_inc(n1T_in_psum, 1)

            def turn_n2(c):
                s = c % 2
                pe.wait_ge(n_ready[1], c + 1)
                if c >= 1:
                    pe.wait_ge(v_part_ready, c)
                else:
                    pe.wait_ge(bT_ready, 1)
                for j in range(STEPS):
                    last = turn(p_t2[:, j * D:(j + 1) * D], n2[:, s, j * D:(j + 1) * D], NB)
                last.then_inc(n2T_in_psum, 1)

            def state_inputs(c):
                s = c % 2
                pe.wait_ge(uT_ready, c + 1)
                if c == 0:
                    pe.wait_ge(bT_ready, 1)
                    pe.wait_ge(condT_ready, 1)
                else:
                    pe.wait_ge(z_ready, STEPS * c)
                for half in range(2):
                    rows = slice(half * R, (half + 1) * R)
                    pe.matmul(p_b[rows, 0:HB], bT[:, 0, :], uT[:, s, half * HB:(half + 1) * HB],
                              start=True, stop=(c == 0))
                if c >= 1:
                    if c == 1:
                        pe.wait_ge(next_frame_ready, 1)
                    for half in range(2):
                        rows = slice(half * R, (half + 1) * R)
                        pe.matmul(p_b[rows, 0:HB], next_frame[rows, :], z[rows, c - 1, STEPS - 1, :],
                                  start=False, stop=True)
                for j in range(1, STEPS):
                    for half in range(2):
                        rows = slice(half * R, (half + 1) * R)
                        at = j * NB + half * HB
                        last = pe.matmul(p_b[rows, j * HB:(j + 1) * HB], bT[:, j, :], uT[:, s, at:at + HB],
                                         start=True, stop=True)
                last.then_inc(b_done, 1)

            def state_outputs(c):
                pe.wait_ge(z_ready, STEPS * (c + 1))
                if c == 0:
                    pe.wait_ge(c_turned_ready, 1)
                    pe.wait_ge(gates_ready, 1)
                else:
                    pe.wait_ge(gated_ready, c)
                for j in range(STEPS):
                    for half in range(2):
                        rows = slice(half * R, (half + 1) * R)
                        last = pe.matmul(p_c[rows, j * D:(j + 1) * D], z[rows, c, j, :], c_turned[rows, j, :],
                                         start=True, stop=True)
                last.then_inc(c_done, 1)

            def hidden(c):
                s = c % 2
                pe.wait_ge(v_hi_ready, c + 1)
                pe.wait_ge(v_lo_ready, c + 1)
                if c == 0:
                    pe.wait_ge(w1_split, 1)
                for f in range(NF):
                    if NF * c + f >= 2:
                        pe.wait_ge(h_ready, NF * c + f - 1)
                    elif f == 0:
                        pe.wait_ge(scale1_ready, 1)
                    else:
                        pe.wait_ge(scale2_ready, 1)
                    tile = slice(f * D, (f + 1) * D)
                    pe.matmul(p_h[f % 2][:, :], w1_lo[:, tile], v_hi[:, s, :], start=True, stop=False)
                    pe.matmul(p_h[f % 2][:, :], w1_hi[:, tile], v_lo[:, s, :], start=False, stop=False)
                    pe.matmul(p_h[f % 2][:, :], w1_hi[:, tile], v_hi[:, s, :], start=False, stop=True) \
                      .then_inc(w1_done, 1)

            def feed_forward(c, js):
                s = c % 2
                if js[0] == 0:
                    pe.wait_ge(h_ready, NF * (c + 1))
                    if c == 0:
                        pe.wait_ge(w2_landed, 16)
                        pe.wait_ge(gates_ready, 1)
                    elif c == 1:
                        pe.wait_ge(b1_col_ready, 1)
                        pe.wait_ge(cT_ready, 1)
                    else:
                        pe.wait_ge(gated_ff_ready, c - 1)
                for j in js:
                    for f in range(NF):
                        last = pe.matmul(p_y[s][:, j * D:(j + 1) * D], h[:, s, f, j * NB:(j + 1) * NB],
                                         w2_sb[:, f, :], start=(f == 0), stop=(f == NF - 1))
                if js[-1] == STEPS - 1:
                    last.then_inc(w2_done, 1)

            for i in range(-2, NC):
                if 0 <= i + 1 < NC:
                    state_outputs(i + 1)
                if 0 <= i < NC:
                    hidden(i)
                if 0 <= i + 2 < NC:
                    turn_n1(i + 2)
                if 0 <= i < NC:
                    feed_forward(i, [0, 1])
                if 0 <= i + 2 < NC:
                    state_inputs(i + 2)
                if 0 <= i + 1 < NC:
                    turn_n2(i + 1)
                if 0 <= i < NC:
                    feed_forward(i, [2, 3])


_INS = ['x', 'cond_1024', 'L0_cond_Wm', 'L0_cond_bm', 'L0_cond_Lam_re', 'L0_cond_Lam_im', 'L0_cond_B_re',
        'L0_cond_B_im', 'L0_cond_C_re', 'L0_cond_C_im', 'L0_cond_D_diag', 'L0_cond_log_step', 'L0_cond_Wc',
        'L0_cond_bc', 'L0_cond_W1', 'L0_cond_b1', 'L0_cond_W2', 'L0_cond_b2']
_OUTS = [((128, 32, 128), 'float32')]


def kernel(**inputs):
    import numpy as _np
    import concourse.bacc as _bacc
    from concourse import mybir as _mybir
    from concourse.bass_utils import run_bass_kernel_spmd as _run

    nc = _bacc.Bacc("TRN2", target_bir_lowering=False, num_devices=1)
    arrays, args = {}, []
    for name in _INS:
        a = _np.ascontiguousarray(inputs[name])
        arrays[f"in_{name}_dram"] = a
        args.append(nc.dram_tensor(f"in_{name}_dram", a.shape, _mybir.dt.from_np(a.dtype), kind="ExternalInput").ap())
    for i, (shape, dtype) in enumerate(_OUTS):
        dt = _mybir.dt.from_np(_np.dtype(dtype))
        args.append(nc.dram_tensor(f"out_{i}_dram", shape, dt, kind="ExternalOutput").ap())
    conditioned_s5_block(nc, *args)
    r = _run(nc, [arrays], core_ids=[0])
    return r.results[0]["out_0_dram"]
```

```python
from contextlib import ExitStack

import numpy as np

import concourse.bass as bass
from concourse import mybir

ALU = mybir.AluOpType
ACT = mybir.ActivationFunctionType
F32 = mybir.dt.float32
F32R = mybir.dt.float32r
I32 = mybir.dt.int32

STEPS = 4
RING = 3
LO_ROW = 32
PSUM_COLUMNS = 512

SERIES = [1.0, 1 / 2, 1 / 6, 1 / 24, 1 / 120, 1 / 720, 1 / 5040, 1 / 40320]
ROUND = 1.5 * 2.0 ** 23
LOG2E = float(np.log2(np.e))
LN2_HI = 0.693359375
LN2_LO = float(np.log(2.0) - LN2_HI)
TWO_PI_HI = 6.28125
TWO_PI_MID = float(np.float32(2 * np.pi - TWO_PI_HI))
TWO_PI_LO = float(2 * np.pi - TWO_PI_HI - TWO_PI_MID)
PI_BELOW = 3.1415925
EXP_FLOOR = -87.0
LN_EPS = 1e-5


def conditioned_s5_block(nc, x, cond, Wm, bm, Lam_re, Lam_im, B_re, B_im, C_re, C_im, D_diag,
                         log_step, Wc, bc, W1, b1, W2, b2, out):
    NB, L, D = x.shape
    P = Lam_re.shape[0]
    FF = W1.shape[1]
    NC = L // STEPS
    NF = FF // D
    CW = STEPS * D
    HB = NB // 2
    R = 2 * P
    assert NB == D == 128 and P == 32 and CW == PSUM_COLUMNS and NF * D == FF

    with ExitStack() as ctx:
        def sb(name, shape, dt=F32):
            return ctx.enter_context(nc.sbuf_tensor(name, shape, dt))

        def bank(name):
            return ctx.enter_context(nc.psum_tensor(name, [128, PSUM_COLUMNS], F32))

        def sem(name):
            return ctx.enter_context(nc.semaphore(name))

        cond_sb = sb("cond_sb", [NB, D])
        condT = sb("condT", [D, NB])
        wmod = sb("wmod", [D, 8 * D])
        mod_bias = sb("mod_bias", [1, 8 * D])
        d_row = sb("d_row", [1, D])
        ones_row = sb("ones_row", [1, 128])
        ident = sb("ident", [128, 128])
        same_part = sb("same_part", [128, R])
        other_part = sb("other_part", [128, R])
        b1_rows = sb("b1_rows", [NF, D])
        b1_col = sb("b1_col", [D, NF])
        w1_sb = sb("w1_sb", [D, FF])
        w1_hi = sb("w1_hi", [D, FF], F32R)
        w1_lo = sb("w1_lo", [D, FF], F32R)
        w2_sb = sb("w2_sb", [D, NF, D])
        b2_rows = sb("b2_rows", [LO_ROW + 1, STEPS, D])
        b2_hi = sb("b2_hi", [LO_ROW + 1, CW], F32R)
        b2_parts = sb("b2_parts", [128, CW], F32R)
        ones = sb("ones", [128, NB], F32R)
        scale1 = sb("scale1", [NB, D])
        shift1 = sb("shift1", [NB, D])
        scale_ff = sb("scale_ff", [NB, D])
        scale2 = sb("scale2", [NB, D])
        shift2a = sb("shift2a", [NB, D])
        shift2 = sb("shift2", [NB, D])
        gate_a = sb("gate_a", [NB, D])
        gate_d = sb("gate_d", [NB, D])
        gate_ff = sb("gate_ff", [NB, D])

        lam = sb("lam", [128, 3])
        series_even = sb("series_even", [128, 4])
        series_odd = sb("series_odd", [128, 4])
        step_no = sb("step_no", [128, STEPS + 1])
        sign = sb("sign", [128, 1])
        small = sb("small", [128, 160])
        first_sine = sb("first_sine", [1, 1])
        first_gelu = sb("first_gelu", [1, 1])
        angles = sb("angles", [128, 2, STEPS + 1])
        sines = sb("sines", [128, 2, STEPS + 1])
        b_parts = sb("b_parts", [R, D])
        factor_part = sb("factor_part", [128, STEPS + 1, R])
        factor_part2 = sb("factor_part2", [128, STEPS + 1, R])
        factors = sb("factors", [128, STEPS + 1, R])
        bT = sb("bT", [D, STEPS, R])
        c_parts = sb("c_parts", [D, 5, P])
        cT = sb("cT", [128, 2, D])
        c_im = sb("c_im", [128, STEPS + 1])
        c_part = sb("c_part", [128, STEPS, D])
        c_turned = sb("c_turned", [128, STEPS, D])

        x_sb = sb("x_sb", [NB, NC, CW])
        n1 = sb("n1", [NB, RING, CW])
        u_part = sb("u_part", [NB, RING, CW])
        u = sb("u", [NB, RING, CW])
        uT = sb("uT", [D, RING, CW])
        z = sb("z", [128, NC, STEPS, HB])
        skip_part = sb("skip_part", [NB, RING, CW])
        skip = sb("skip", [NB, RING, CW])
        gated = sb("gated", [NB, RING, CW])
        y1 = sb("y1", [NB, NC, CW])
        n2 = sb("n2", [NB, RING, CW])
        w_part = sb("w_part", [NB, RING, CW])
        w = sb("w", [NB, RING, CW])
        v_hi = sb("v_hi", [D, RING, CW], F32R)
        v_lo = sb("v_lo", [D, RING, CW], F32R)
        h = sb("h", [D, 2, NF, CW])
        gated_ff = sb("gated_ff", [NB, RING, CW])
        y2 = sb("y2", [NB, NC, CW])
        raw_stats = [sb(f"raw_stats{k}", [NB, NC, STEPS, 6]) for k in (1, 2)]
        mean_var = [sb(f"mean_var{k}", [NB, NC, STEPS, 2]) for k in (1, 2)]
        var_eps = [sb(f"var_eps{k}", [NB, NC, STEPS]) for k in (1, 2)]
        neg_mean = [sb(f"neg_mean{k}", [NB, NC, STEPS]) for k in (1, 2)]
        rstd = [sb(f"rstd{k}", [NB, NC, STEPS]) for k in (1, 2)]
        norm_bias = [sb(f"norm_bias{k}", [NB, NC, STEPS]) for k in (1, 2)]

        minus_half = sb("minus_half", [NB, STEPS])

        p_t1, p_t2, p_b, p_c = bank("p_t1"), bank("p_t2"), bank("p_b"), bank("p_c")
        p_h = [bank("p_h0"), bank("p_h1")]
        p_y = [bank("p_y0"), bank("p_y1")]

        x_landed = [sem(f"x_landed{c}") for c in range(NC)]
        log_step_landed, lam_landed, b_landed, c_landed = (sem("log_step_landed"), sem("lam_landed"), sem("b_landed"),
                                                           sem("c_landed"))
        cond_landed, wmod_a_landed, wmod_landed = sem("cond_landed"), sem("wmod_a_landed"), sem("wmod_landed")
        wc_landed, bm_landed, bc_landed, d_landed = (sem("wc_landed"), sem("bm_landed"), sem("bc_landed"),
                                                     sem("d_landed"))
        w1_landed, w2_landed, b1_landed, b2_landed = (sem("w1_landed"), sem("w2_landed"), sem("b1_landed"),
                                                      sem("b2_landed"))
        const_chain, ident_ready, const_ready = sem("const_chain"), sem("ident_ready"), sem("const_ready")
        ones_ready, b2_zeroed, b2_ready = sem("ones_ready"), sem("b2_zeroed"), sem("b2_ready")
        b2_hi_ready = sem("b2_hi_ready")
        chain = sem("chain")
        angles_ready, sines_ready = sem("angles_ready"), sem("sines_ready")
        turns_ready, bT_in_psum, bT_ready = sem("turns_ready"), sem("bT_in_psum"), sem("bT_ready")
        cT_in_psum, cT_ready, b1_col_ready = sem("cT_in_psum"), sem("cT_ready"), sem("b1_col_ready")
        c_im_ready, c_part_ready, c_turned_ready = sem("c_im_ready"), sem("c_part_ready"), sem("c_turned_ready")
        condT_in_psum, condT_ready = sem("condT_in_psum"), sem("condT_ready")
        mod_a_in_psum, mod_b_in_psum = sem("mod_a_in_psum"), sem("mod_b_in_psum")
        mod_c_in_psum = sem("mod_c_in_psum")
        modulation1_ready, gates_ready, modulation2_ready = (sem("modulation1_ready"), sem("gates_ready"),
                                                             sem("modulation2_ready"))
        w1_split = sem("w1_split")
        raw_ready, stats_ready = [sem("raw1_ready"), sem("raw2_ready")], [sem("stats1_ready"), sem("stats2_ready")]
        var_eps_ready = [sem("var_eps1_ready"), sem("var_eps2_ready")]
        power_ready = [sem("power1_ready"), sem("power2_ready")]
        rstd_ready = [sem("rstd1_ready"), sem("rstd2_ready")]
        n_ready = [sem("n1_ready"), sem("n2_ready")]
        u_part_ready, u_ready = sem("u_part_ready"), sem("u_ready")
        u_in_psum, uT_ready = sem("u_in_psum"), sem("uT_ready")
        b_done, z_ready = sem("b_done"), sem("z_ready")
        c_done = sem("c_done")
        skip_part_ready, skip_ready = sem("skip_part_ready"), sem("skip_ready")
        gated_ready, y1_ready = sem("gated_ready"), sem("y1_ready")
        w_part_ready, w_ready, w_in_psum = sem("w_part_ready"), sem("w_ready"), sem("w_in_psum")
        v_hi_ready, v_lo_ready = sem("v_hi_ready"), sem("v_lo_ready")
        w1_done, h_ready, w2_done = sem("w1_done"), sem("h_ready"), sem("w2_done")
        gated_ff_ready, y2_ready, stored = sem("gated_ff_ready"), sem("y2_ready"), sem("stored")

        def over_steps(table):
            return table[:, :].unsqueeze(1).to_broadcast([128, STEPS, 128])

        def steps(ap):
            return ap.rearrange("p (s d) -> p s d", s=STEPS)

        def run(stages):
            for i in range(-max(ahead for _, ahead in stages), NC - min(ahead for _, ahead in stages)):
                for stage, ahead in stages:
                    if 0 <= i + ahead < NC:
                        stage(i + ahead)

        def after_first(stage):
            return lambda c: stage(c) if c >= 1 else None

        block = ctx.enter_context(nc.Block())

        @block.sync
        def _(sp):
            def load_x(c):
                sp.dma_start(x_sb[:, c, :], x[:, c * STEPS:(c + 1) * STEPS, :].rearrange("b s d -> b (s d)")) \
                  .then_inc(x_landed[c], 16)

            def load_lam(source, k, landed):
                sp.dma_start(lam[:, k:k + 1], source.rearrange("(g p o) -> g p o", g=1, o=1)
                             .broadcast_to([4, P, 1])).then_inc(landed, 16)

            load_lam(log_step, 2, log_step_landed)
            load_x(0)
            load_lam(Lam_im, 1, lam_landed)
            load_lam(Lam_re, 0, lam_landed)
            sp.dma_start(mod_bias[:, 0:6 * D], bm.rearrange("(o n) -> o n", o=1)).then_inc(bm_landed, 16)
            sp.dma_start(wmod[:, 2 * D:6 * D], Wm[:, 2 * D:6 * D]).then_inc(wmod_landed, 16)
            sp.dma_start(wmod[:, 6 * D:8 * D], Wc).then_inc(wc_landed, 16)
            sp.dma_start(b_parts[0:P, :], B_re).then_inc(b_landed, 16)
            sp.dma_start(b_parts[P:R, :], B_im).then_inc(b_landed, 16)
            sp.dma_start(c_parts[:, 0::2, :], C_re.rearrange("d (o p) -> d o p", o=1).broadcast_to([D, 3, P])) \
              .then_inc(c_landed, 16)
            sp.dma_start(c_parts[:, 1::2, :], C_im.rearrange("d (o p) -> d o p", o=1).broadcast_to([D, 2, P])) \
              .then_inc(c_landed, 16)
            load_x(1)
            sp.dma_start(w1_sb[:, :], W1).then_inc(w1_landed, 16)
            load_x(2)
            sp.dma_start(w2_sb[:, :, :], W2.rearrange("(f k) d -> k f d", k=D)).then_inc(w2_landed, 16)
            for c in range(3, NC):
                load_x(c)
            for c in range(NC):
                sp.wait_ge(y2_ready, c + 1)
                sp.dma_start(out[:, c * STEPS:(c + 1) * STEPS, :].rearrange("b s d -> b (s d)"), y2[:, c, :]) \
                  .then_inc(stored, 16)
            sp.wait_ge(stored, 16 * NC)

        @block.gpsimd
        def _(pool):
            count = {"const": 0}

            def const_link(ins):
                count["const"] += 1
                ins.then_inc(const_chain, 1)
                pool.wait_ge(const_chain, count["const"])

            def mark(table, offsets):
                for at in offsets:
                    ins = pool.affine_select(out=table[:, :], in_=table[:, :], compare_op=ALU.not_equal, fill=1.0,
                                             base=-at, pattern=[[-1, table.shape[1]]], channel_multiplier=1)
                    if at != offsets[-1]:
                        const_link(ins)
                return ins

            def rstd_of(k, c):
                pool.wait_ge(stats_ready[k], c + 1)
                pool.tensor_scalar(var_eps[k][:, c, :], mean_var[k][:, c, :, 1], LN_EPS, None, ALU.add) \
                    .then_inc(var_eps_ready[k], 1)
                pool.tensor_scalar(neg_mean[k][:, c, :], mean_var[k][:, c, :, 0], -1.0, None, ALU.mult)
                pool.wait_ge(var_eps_ready[k], c + 1)
                pool.tensor_tensor(rstd[k][:, c, :], var_eps[k][:, c, :], minus_half[:, :], ALU.pow) \
                    .then_inc(power_ready[k], 1)
                pool.wait_ge(power_ready[k], c + 1)
                pool.tensor_tensor(norm_bias[k][:, c, :], neg_mean[k][:, c, :], rstd[k][:, c, :], ALU.mult) \
                    .then_inc(rstd_ready[k], 1)

            def scale_u(c):
                s = c % RING
                if c == 0:
                    pool.wait_ge(modulation1_ready, 1)
                if c >= RING:
                    pool.wait_ge(u_ready, c - RING + 1)
                pool.wait_ge(n_ready[0], c + 1)
                pool.tensor_tensor(steps(u_part[:, s, :]), steps(n1[:, s, :]), over_steps(scale1), ALU.mult) \
                    .then_inc(u_part_ready, 1)

            def shift_u(c):
                s = c % RING
                if c >= RING:
                    pool.wait_ge(u_in_psum, c - RING + 1)
                    pool.wait_ge(skip_part_ready, c - RING + 1)
                pool.wait_ge(u_part_ready, c + 1)
                pool.tensor_tensor(steps(u[:, s, :]), steps(u_part[:, s, :]), over_steps(shift1), ALU.add) \
                    .then_inc(u_ready, 1)

            def scale_skip(c):
                s = c % RING
                if c == 0:
                    pool.wait_ge(gates_ready, 1)
                if c >= RING:
                    pool.wait_ge(skip_ready, c - RING + 1)
                pool.wait_ge(u_ready, c + 1)
                pool.tensor_tensor(steps(skip_part[:, s, :]), steps(u[:, s, :]), over_steps(gate_d), ALU.mult) \
                    .then_inc(skip_part_ready, 1)

            def add_skip(c):
                s = c % RING
                if c >= RING:
                    pool.wait_ge(y1_ready, c - RING + 1)
                pool.wait_ge(skip_part_ready, c + 1)
                pool.tensor_tensor(skip[:, s, :], skip_part[:, s, :], x_sb[:, c, :], ALU.add).then_inc(skip_ready, 1)

            const_link(pool.memset(ident[:, :], 0.0))
            mark(ident, [0]).then_inc(ident_ready, 1)
            pool.memset(minus_half[:, :], -0.5)
            pool.memset(same_part[:, :], 0.0)
            const_link(pool.memset(other_part[:, :], 0.0))
            mark(same_part, [0, R]).then_inc(const_ready, 1)
            mark(other_part, [-P, P, 3 * P]).then_inc(const_ready, 1)
            pool.dma_start(d_row[:, :], D_diag.rearrange("(o n) -> o n", o=1)).then_inc(d_landed, 16)
            pool.dma_start(mod_bias[:, 6 * D:8 * D], bc.rearrange("(o n) -> o n", o=1)).then_inc(bc_landed, 16)
            pool.dma_start(b1_rows[:, :], b1.rearrange("(f d) -> f d", f=NF)).then_inc(b1_landed, 16)
            rstd_of(0, 0)
            for row in (0, LO_ROW):
                pool.dma_start(b2_rows[row:row + 1, :, :],
                               b2.rearrange("(o s n) -> o s n", o=1, s=1).broadcast_to([1, STEPS, D])) \
                    .then_inc(b2_landed, 16)
            pool.memset(ones[:, :].bitcast(F32), 1.0)
            pool.memset(b2_parts[:, :].bitcast(F32), 0.0).then_inc(b2_zeroed, 1)

            scale_u(0)
            shift_u(0)
            scale_skip(0)
            add_skip(0)

            def rstd1(c):
                rstd_of(0, c)

            def rstd2(c):
                rstd_of(1, c)

            rstd1, scale_u, shift_u, scale_skip, add_skip = map(after_first, (rstd1, scale_u, shift_u, scale_skip,
                                                                              add_skip))

            run([(shift_u, 1), (add_skip, 0), (rstd1, 2), (scale_skip, 1), (rstd2, 0), (scale_u, 2)])

        @block.vector
        def _(dve):
            count = {"chain": 0}

            def note(ins):
                count["chain"] += 1
                return ins.then_inc(chain, 1)

            def link(ins):
                note(ins)
                dve.wait_ge(chain, count["chain"])

            cells = iter(range(160))

            def cell(width=1):
                at = [next(cells) for _ in range(width)]
                return small[:, at[0]:at[-1] + 1]

            def raw_stats_of(k, c, js=range(STEPS)):
                if js[0] == 0:
                    if k == 0:
                        dve.wait_ge(x_landed[c], 16)
                    else:
                        dve.wait_ge(y1_ready, c + 1)
                src = x_sb if k == 0 else y1
                for j in js:
                    ins = dve.bn_stats(raw_stats[k][:, c, j, :], src[:, c, j * D:(j + 1) * D])
                if js[-1] == STEPS - 1:
                    ins.then_inc(raw_ready[k], 1)

            def mean_var_of(k, c):
                dve.wait_ge(raw_ready[k], c + 1)
                for j in range(STEPS):
                    ins = dve.bn_aggr(mean_var[k][:, c, j, :], raw_stats[k][:, c, j, :])
                ins.then_inc(stats_ready[k], 1)

            dve.memset(ones_row[:, :], 1.0).then_inc(ones_ready, 1)
            for k in range(4):
                dve.memset(series_even[:, k:k + 1], SERIES[2 * k])
                dve.memset(series_odd[:, k:k + 1], SERIES[2 * k + 1])
            for j in range(STEPS + 1):
                dve.memset(step_no[:, j:j + 1], float(j))
            link(dve.memset(sign[:, :], 1.0))
            dve.memset(sign[0:P, :], -1.0)
            note(dve.memset(sign[2 * P:3 * P, :], -1.0))

            lam_re, lam_im, log_dt = (lam[:, k:k + 1] for k in range(3))
            W = STEPS + 1

            clamped, shifted, whole, f1, f, power = (cell() for _ in range(6))
            f2, f4, s4, s2, s1, f_power = cell(), cell(), cell(4), cell(2), cell(), cell()
            dve.wait_ge(log_step_landed, 16)
            note(dve.tensor_scalar(shifted, log_dt, LOG2E, ROUND, ALU.mult, ALU.add))
            link(dve.tensor_scalar(clamped, log_dt, EXP_FLOOR, None, ALU.max))
            link(dve.tensor_scalar(whole, shifted, ROUND, -126.0, ALU.subtract, ALU.max))
            link(dve.scalar_tensor_tensor(f1, whole, -LN2_HI, clamped, ALU.mult, ALU.add))
            note(dve.tensor_scalar(power.bitcast(I32), whole, 127.0, 2.0 ** 23, ALU.add, ALU.mult))
            link(dve.scalar_tensor_tensor(f, whole, -LN2_LO, f1, ALU.mult, ALU.add))
            note(dve.scalar_tensor_tensor(s4, series_odd[:, :], f, series_even[:, :], ALU.mult, ALU.add))
            link(dve.tensor_tensor(f2, f, f, ALU.mult))
            note(dve.scalar_tensor_tensor(s2, s4[:, 1::2], f2, s4[:, 0::2], ALU.mult, ALU.add))
            note(dve.tensor_tensor(f4, f2, f2, ALU.mult))
            link(dve.tensor_tensor(f_power, f, power, ALU.mult))
            note(dve.scalar_tensor_tensor(s1, s2[:, 1:2], f4, s2[:, 0:1], ALU.mult, ALU.add))
            dt, theta, decay_log, sq_im, norm2, inv_norm2 = (cell() for _ in range(6))
            raw_stats_of(0, 0, [0, 1])
            dve.wait_ge(chain, count["chain"])
            note(dve.scalar_tensor_tensor(dt, s1, f_power, power, ALU.mult, ALU.add))
            raw_stats_of(0, 0, [2, 3])
            dve.wait_ge(chain, count["chain"])
            dve.wait_ge(lam_landed, 32)
            note(dve.tensor_tensor(theta, lam_im, dt, ALU.mult))
            note(dve.tensor_tensor(sq_im, lam_im, lam_im, ALU.mult))
            note(dve.tensor_scalar(decay_log, lam_re, dt, EXP_FLOOR, ALU.mult, ALU.max))
            mean_var_of(0, 0)
            dve.wait_ge(chain, count["chain"])

            angle, rounds_s, rounds, a1, a2, a3 = (cell(W) for _ in range(6))
            shifted, whole, f1, f, power, power_m1 = (cell() for _ in range(6))
            f2, f4, s4, s2, s1, f_power = cell(), cell(), cell(4), cell(2), cell(), cell()
            decay, decay_m1, ratio_re, ratio_im = (cell() for _ in range(4))
            note(dve.tensor_scalar(angle, step_no[:, :], theta, None, ALU.mult))
            note(dve.tensor_scalar(shifted, decay_log, LOG2E, ROUND, ALU.mult, ALU.add))
            link(dve.scalar_tensor_tensor(norm2, lam_re, lam_re, sq_im, ALU.mult, ALU.add))
            link(dve.tensor_scalar(rounds_s, angle, float(1 / (2 * np.pi)), ROUND, ALU.mult, ALU.add))
            note(dve.tensor_scalar(rounds, rounds_s, ROUND, None, ALU.subtract))
            link(dve.tensor_scalar(whole, shifted, ROUND, None, ALU.subtract))
            note(dve.scalar_tensor_tensor(a1, rounds, -TWO_PI_HI, angle, ALU.mult, ALU.add))
            link(dve.scalar_tensor_tensor(f1, whole, -LN2_HI, decay_log, ALU.mult, ALU.add))
            note(dve.scalar_tensor_tensor(a2, rounds, -TWO_PI_MID, a1, ALU.mult, ALU.add))
            link(dve.scalar_tensor_tensor(f, whole, -LN2_LO, f1, ALU.mult, ALU.add))
            note(dve.scalar_tensor_tensor(a3, rounds, -TWO_PI_LO, a2, ALU.mult, ALU.add))
            link(dve.tensor_scalar(power.bitcast(I32), whole, 127.0, 2.0 ** 23, ALU.add, ALU.mult))
            note(dve.tensor_scalar(angles[:, 0, :], a3, -PI_BELOW, PI_BELOW, ALU.max, ALU.min))
            note(dve.scalar_tensor_tensor(s4, series_odd[:, :], f, series_even[:, :], ALU.mult, ALU.add))
            link(dve.tensor_tensor(f2, f, f, ALU.mult))
            dve.tensor_scalar(angles[:, 1, :], angles[:, 0, :], 0.5, None, ALU.mult).then_inc(angles_ready, 1)
            note(dve.tensor_tensor(f4, f2, f2, ALU.mult))
            note(dve.scalar_tensor_tensor(s2, s4[:, 1::2], f2, s4[:, 0::2], ALU.mult, ALU.add))
            note(dve.tensor_tensor(f_power, f, power, ALU.mult))
            note(dve.tensor_scalar(power_m1, power, -1.0, None, ALU.add))
            link(dve.reciprocal(inv_norm2, norm2))
            note(dve.scalar_tensor_tensor(s1, s2[:, 1:2], f4, s2[:, 0:1], ALU.mult, ALU.add))
            note(dve.tensor_tensor(ratio_re, lam_re, inv_norm2, ALU.mult))
            link(dve.tensor_tensor(ratio_im, lam_im, inv_norm2, ALU.mult))
            note(dve.scalar_tensor_tensor(decay, s1, f_power, power, ALU.mult, ALU.add))
            note(dve.scalar_tensor_tensor(decay_m1, s1, f_power, power_m1, ALU.mult, ALU.add))

            dve.wait_ge(mod_b_in_psum, 1)
            link(dve.tensor_copy(gate_a[:, :], p_h[0][:, 0:D]))
            dve.tensor_tensor(gate_d[:, :], gate_a[:, :], p_h[0][:, 2 * D:3 * D], ALU.mult).then_inc(gates_ready, 1)

            sin, sin_half = sines[:, 0, :], sines[:, 1, :]
            half_sq, cos, minus_sin, sign_cos, sign_sin, w_re_a, w_im_a = (cell(W) for _ in range(7))
            c_re = cell(W)
            w_re, w_im = cell(W), cell(W)
            cos_m1, num_re, num_im, t1, t2, q_re, minus_q_im = (cell() for _ in range(7))
            dve.wait_ge(chain, count["chain"])
            dve.wait_ge(sines_ready, 1)
            note(dve.tensor_tensor(half_sq, sin_half, sin_half, ALU.mult))
            note(dve.tensor_tensor(num_im, decay, sin[:, 1:2], ALU.mult))
            note(dve.tensor_scalar(minus_sin, sin, -1.0, None, ALU.mult))
            link(dve.tensor_scalar(sign_sin, sin, sign[:, 0:1], None, ALU.mult))
            dve.tensor_scalar(c_im[:, :], sin, -2.0, None, ALU.mult).then_inc(c_im_ready, 1)
            note(dve.tensor_scalar(cos_m1, half_sq[:, 1:2], -2.0, None, ALU.mult))
            note(dve.tensor_scalar(cos, half_sq, -2.0, 1.0, ALU.mult, ALU.add))
            note(dve.tensor_tensor(t1, num_im, ratio_im, ALU.mult))
            link(dve.tensor_tensor(t2, num_im, ratio_re, ALU.mult))
            note(dve.scalar_tensor_tensor(num_re, decay_m1, cos[:, 1:2], cos_m1, ALU.mult, ALU.add))
            note(dve.tensor_tensor(w_re[:, STEPS:W], decay, cos[:, STEPS:W], ALU.mult))
            note(dve.scalar_tensor_tensor(w_im[:, STEPS:W], sign_sin[:, STEPS:W], -1.0, decay, ALU.mult, ALU.mult))
            link(dve.tensor_scalar(sign_cos, cos, sign[:, 0:1], None, ALU.mult))
            note(dve.scalar_tensor_tensor(q_re, num_re, ratio_re, t1, ALU.mult, ALU.add))
            link(dve.scalar_tensor_tensor(minus_q_im, num_re, ratio_im, t2, ALU.mult, ALU.subtract))
            note(dve.tensor_scalar(c_re, sign_cos, -2.0, None, ALU.mult))
            note(dve.tensor_scalar(w_re_a[:, 0:STEPS], cos[:, 0:STEPS], q_re, None, ALU.mult))
            link(dve.tensor_scalar(w_im_a[:, 0:STEPS], sign_sin[:, 0:STEPS], q_re, None, ALU.mult))
            note(dve.scalar_tensor_tensor(w_im[:, 0:STEPS], sign_cos[:, 0:STEPS], minus_q_im, w_im_a[:, 0:STEPS],
                                          ALU.mult, ALU.add))
            link(dve.scalar_tensor_tensor(w_re[:, 0:STEPS], minus_sin[:, 0:STEPS], minus_q_im, w_re_a[:, 0:STEPS],
                                          ALU.mult, ALU.add))
            by_row = [128, W, R]
            dve.wait_ge(const_ready, 2)
            note(dve.tensor_tensor(factor_part[:, :, :], same_part[:, :].unsqueeze(1).to_broadcast(by_row),
                                   w_re.unsqueeze(2).to_broadcast(by_row), ALU.mult))
            link(dve.tensor_tensor(factor_part2[:, :, :], other_part[:, :].unsqueeze(1).to_broadcast(by_row),
                                   w_im.unsqueeze(2).to_broadcast(by_row), ALU.mult))
            dve.tensor_tensor(factors[:, :, :], factor_part[:, :, :], factor_part2[:, :, :], ALU.add) \
               .then_inc(turns_ready, 1)

            def turn_c():
                dve.wait_ge(c_part_ready, 1)
                for j in range(STEPS):
                    ins = dve.scalar_tensor_tensor(c_turned[:, j, :], cT[:, 0, :], c_re[:, j:j + 1], c_part[:, j, :],
                                                   ALU.mult, ALU.add)
                ins.then_inc(c_turned_ready, 1)

            def copy_bT():
                dve.wait_ge(bT_in_psum, 1)
                dve.tensor_copy(bT[:, :, :], p_t2[:, 0:STEPS * R].rearrange("p (s r) -> p s r", s=STEPS)) \
                   .then_inc(bT_ready, 1)

            def second_modulation():
                dve.wait_ge(mod_c_in_psum, 1)
                note(dve.tensor_copy(gate_ff[:, :], p_h[1][:, D:2 * D]))
                link(dve.tensor_scalar(scale_ff[:, :], p_h[1][:, 0:D], 1.0, None, ALU.add))
                note(dve.scalar_tensor_tensor(scale2[:, :], p_h[1][:, 2 * D:3 * D], 1.0, scale_ff[:, :],
                                              ALU.add, ALU.mult))
                link(dve.tensor_tensor(shift2a[:, :], p_h[1][:, 3 * D:4 * D], scale_ff[:, :], ALU.mult))
                dve.tensor_tensor(shift2[:, :], p_h[0][:, D:2 * D], shift2a[:, :], ALU.add) \
                   .then_inc(modulation2_ready, 1)

            def split_w1():
                dve.wait_ge(w1_landed, 16)
                link(dve.tensor_copy(w1_hi[:, :], w1_sb[:, :]))
                dve.tensor_tensor(w1_lo[:, :], w1_sb[:, :], w1_hi[:, :].bitcast(F32), ALU.subtract) \
                   .then_inc(w1_split, 1)

            def split_b2():
                dve.wait_ge(b2_hi_ready, 1)
                low = slice(LO_ROW, LO_ROW + 1)
                dve.tensor_tensor(b2_parts[low, :], b2_rows[low, :, :].rearrange("p s d -> p (s d)"),
                                  b2_hi[low, :].bitcast(F32), ALU.subtract).then_inc(b2_ready, 1)

            def recur(j):
                def stage(c):
                    if j == 0:
                        dve.wait_ge(b_done, c + 1)
                        ins = dve.tensor_copy(z[:, c, 0, :], p_b[:, 0:HB])
                    else:
                        dve.wait_ge(z_ready, STEPS * c + j)
                        ins = dve.scalar_tensor_tensor(z[:, c, j, :], z[:, c, j - 1, :], decay,
                                                       p_b[:, j * HB:(j + 1) * HB], ALU.mult, ALU.add)
                    ins.then_inc(z_ready, 1)
                return stage

            def gate_state(c):
                s = c % RING
                dve.wait_ge(c_done, c + 1)
                if c >= RING:
                    dve.wait_ge(y1_ready, c - RING + 1)
                dve.tensor_tensor(steps(gated[:, s, :]), steps(p_c[:, :]), over_steps(gate_a), ALU.mult) \
                   .then_inc(gated_ready, 1)

            def add_state(c):
                dve.wait_ge(skip_ready, c + 1)
                dve.wait_ge(gated_ready, c + 1)
                dve.tensor_tensor(y1[:, c, :], gated[:, c % RING, :], skip[:, c % RING, :], ALU.add) \
                   .then_inc(y1_ready, 1)

            def scale_w(c):
                s = c % RING
                dve.wait_ge(n_ready[1], c + 1)
                if c >= RING:
                    dve.wait_ge(w_ready, c - RING + 1)
                if c == 0:
                    dve.wait_ge(modulation2_ready, 1)
                dve.tensor_tensor(steps(w_part[:, s, :]), steps(n2[:, s, :]), over_steps(scale2), ALU.mult) \
                   .then_inc(w_part_ready, 1)

            def shift_w(c):
                s = c % RING
                if c >= RING:
                    dve.wait_ge(w_in_psum, c - RING + 1)
                dve.wait_ge(w_part_ready, c + 1)
                dve.tensor_tensor(steps(w[:, s, :]), steps(w_part[:, s, :]), over_steps(shift2), ALU.add) \
                   .then_inc(w_ready, 1)

            def low_v(c):
                s = c % RING
                if c >= RING:
                    dve.wait_ge(w1_done, NF * (c - RING + 1))
                dve.wait_ge(v_hi_ready, c + 1)
                dve.tensor_tensor(v_lo[:, s, :], p_t2[:, :], v_hi[:, s, :].bitcast(F32), ALU.subtract) \
                   .then_inc(v_lo_ready, 1)

            def gate_ff_out(c):
                s = c % RING
                dve.wait_ge(w2_done, c + 1)
                if c >= RING:
                    dve.wait_ge(y2_ready, c - RING + 1)
                dve.tensor_tensor(steps(gated_ff[:, s, :]), steps(p_y[c % 2][:, :]), over_steps(gate_ff), ALU.mult) \
                   .then_inc(gated_ff_ready, 1)

            def add_ff(c):
                dve.wait_ge(gated_ff_ready, c + 1)
                dve.tensor_tensor(y2[:, c, :], gated_ff[:, c % RING, :], y1[:, c, :], ALU.add).then_inc(y2_ready, 1)

            def raw1(c):
                if c >= 2:
                    raw_stats_of(0, c)

            def mean1(c):
                if c >= 2:
                    mean_var_of(0, c)

            def raw2(c):
                raw_stats_of(1, c)

            def mean2(c):
                mean_var_of(1, c)

            z0, z1, z2, z3 = (recur(j) for j in range(STEPS))

            raw_stats_of(0, 1)
            copy_bT()
            mean_var_of(0, 1)
            turn_c()
            for z_step in (z0, z1, z2, z3):
                z_step(0)
            second_modulation()
            split_w1()
            split_b2()
            z0, z1, z2, z3, = map(after_first, (z0, z1, z2, z3))
            run([(add_ff, 0), (mean1, 5), (scale_w, 2), (gate_state, 3), (shift_w, 2), (add_state, 3),
                 (raw2, 3), (low_v, 2), (mean2, 3), (z0, 4), (z1, 4), (z2, 4), (raw1, 6), (z3, 4),
                 (gate_ff_out, 1)])

        @block.scalar
        def _(act):
            act.dma_start(cond_sb[:, :], cond).then_inc(cond_landed, 16)
            act.dma_start(wmod[:, 0:2 * D], Wm[:, 0:2 * D]).then_inc(wmod_a_landed, 16)

            def norm(k, c):
                src, dst = (x_sb, n1) if k == 0 else (y1, n2)
                if c >= RING:
                    act.wait_ge([u_part_ready, w_part_ready][k], c - RING + 1)
                act.wait_ge(rstd_ready[k], c + 1)
                for j in range(STEPS):
                    at = slice(j * D, (j + 1) * D)
                    ins = nc.scalar.activation(dst[:, c % RING, at], src[:, c, at], ACT.Identity,
                                               bias=norm_bias[k][:, c, j:j + 1], scale=rstd[k][:, c, j:j + 1])
                ins.then_inc(n_ready[k], 1)

            def copy_uT(c):
                act.wait_ge(u_in_psum, c + 1)
                if c >= RING:
                    act.wait_ge(b_done, c - RING + 1)
                nc.scalar.copy(uT[:, c % RING, :], p_t1[:, :]).then_inc(uT_ready, 1)

            def high_v(c):
                act.wait_ge(w_in_psum, c + 1)
                if c >= RING:
                    act.wait_ge(w1_done, NF * (c - RING + 1))
                nc.scalar.copy(v_hi[:, c % RING, :], p_t2[:, :]).then_inc(v_hi_ready, 1)

            def gelu(f):
                def stage(c):
                    if f == 0 and c == 0:
                        act.wait_ge(b1_col_ready, 1)
                    if f == 0 and c >= 2:
                        act.wait_ge(w2_done, c - 1)
                    act.wait_ge(w1_done, NF * c + f + 1)
                    nc.scalar.activation(h[:, c % 2, f, :], p_h[f % 2][:, :], ACT.Gelu_apprx_tanh,
                                         bias=b1_col[:, f:f + 1]).then_inc(h_ready, 1)
                return stage

            act.wait_ge(ones_ready, 1)
            nc.scalar.activation(first_sine[:, :], ones_row[:, 0:1], ACT.Sin)
            act.wait_ge(condT_in_psum, 1)
            nc.scalar.copy(condT[:, :], p_b[:, 0:NB]).then_inc(condT_ready, 1)
            norm(0, 0)
            act.wait_ge(angles_ready, 1)
            nc.scalar.activation(sines[:, :, :], angles[:, :, :], ACT.Sin).then_inc(sines_ready, 1)
            nc.scalar.activation(first_gelu[:, :], ones_row[:, 0:1], ACT.Gelu_apprx_tanh)
            act.wait_ge(mod_a_in_psum, 1)
            nc.scalar.activation(scale1[:, :], p_y[0][:, D:2 * D], ACT.Identity, bias=1.0)
            nc.scalar.copy(shift1[:, :], p_y[0][:, 0:D]).then_inc(modulation1_ready, 1)
            act.wait_ge(cT_in_psum, 1)
            nc.scalar.copy(cT[:, :, :], p_y[1][:, 0:2 * D].rearrange("p (k d) -> p k d", k=2)).then_inc(cT_ready, 1)
            nc.scalar.copy(b1_col[:, :], p_y[1][:, 2 * D:2 * D + NF]).then_inc(b1_col_ready, 1)
            act.wait_ge(c_im_ready, 1)
            for j in range(STEPS):
                ins = nc.scalar.activation(c_part[:, j, :], p_y[1][:, D:2 * D], ACT.Identity, scale=c_im[:, j:j + 1])
            ins.then_inc(c_part_ready, 1)
            copy_uT(0)
            flat = b2_rows[:, :, :].rearrange("p s d -> p (s d)")
            act.wait_ge(b2_landed, 32)
            act.wait_ge(b2_zeroed, 1)
            nc.scalar.copy(b2_parts[0:1, :], flat[0:1, :])
            nc.scalar.copy(b2_hi[LO_ROW:LO_ROW + 1, :], flat[LO_ROW:LO_ROW + 1, :]).then_inc(b2_hi_ready, 1)

            def norm1(c):
                if c >= 1:
                    norm(0, c)

            def norm2(c):
                norm(1, c)

            copy_uT = after_first(copy_uT)
            gelu0, gelu1, gelu2, gelu3 = (gelu(f) for f in range(NF))
            run([(norm1, 3), (gelu0, 0), (norm2, 1), (gelu1, 0), (gelu2, 0), (copy_uT, 3), (high_v, 1),
                 (gelu3, 0)])

        @block.tensor
        def _(pe):
            def turn(dst, src, k):
                return pe.transpose(dst, src, ident[0:k, 0:k])

            def modulation(dst, first, width, bias_landed):
                pe.matmul(dst, condT[:, :], wmod[:, first:first + width], start=True, stop=False)
                pe.wait_ge(bias_landed, 16)
                return pe.matmul(dst, ones_row[:, :], mod_bias[:, first:first + width], start=False, stop=True)

            def turn_u(c):
                pe.wait_ge(u_ready, c + 1)
                if c >= 1:
                    pe.wait_ge(uT_ready, c)
                for j in range(STEPS):
                    last = turn(p_t1[:, j * D:(j + 1) * D], u[:, c % RING, j * D:(j + 1) * D], NB)
                last.then_inc(u_in_psum, 1)

            def turn_w(c):
                pe.wait_ge(w_ready, c + 1)
                if c >= 1:
                    pe.wait_ge(v_lo_ready, c)
                for j in range(STEPS):
                    last = turn(p_t2[:, j * D:(j + 1) * D], w[:, c % RING, j * D:(j + 1) * D], NB)
                last.then_inc(w_in_psum, 1)

            halves = [slice(0, R), slice(R, 2 * R)]

            def state_inputs(c):
                pe.wait_ge(uT_ready, c + 1)
                if c == 0:
                    pe.wait_ge(bT_ready, 1)
                else:
                    pe.wait_ge(z_ready, STEPS * c)
                for k, rows in enumerate(halves):
                    last = pe.matmul(p_b[rows, 0:HB], bT[:, 0, :], uT[:, c % RING, k * HB:(k + 1) * HB],
                                     start=True, stop=(c == 0))
                if c >= 1:
                    for rows in halves:
                        pe.matmul(p_b[rows, 0:HB], factors[rows, STEPS, :], z[rows, c - 1, STEPS - 1, :],
                                  start=False, stop=True)
                for j in range(1, STEPS):
                    for k, rows in enumerate(halves):
                        at = j * NB + k * HB
                        last = pe.matmul(p_b[rows, j * HB:(j + 1) * HB], bT[:, j, :], uT[:, c % RING, at:at + HB],
                                         start=True, stop=True)
                last.then_inc(b_done, 1)

            def state_outputs(c):
                pe.wait_ge(z_ready, STEPS * (c + 1))
                if c == 0:
                    pe.wait_ge(c_turned_ready, 1)
                else:
                    pe.wait_ge(gated_ready, c)
                for j in range(STEPS):
                    for rows in halves:
                        last = pe.matmul(p_c[rows, j * D:(j + 1) * D], z[rows, c, j, :], c_turned[rows, j, :],
                                         start=True, stop=True)
                last.then_inc(c_done, 1)

            def hidden(f):
                def stage(c):
                    if f == 0:
                        pe.wait_ge(v_hi_ready, c + 1)
                        pe.wait_ge(v_lo_ready, c + 1)
                        if c == 0:
                            pe.wait_ge(w1_split, 1)
                    hi, lo = v_hi[:, c % RING, :], v_lo[:, c % RING, :]
                    if NF * c + f >= 2:
                        pe.wait_ge(h_ready, NF * c + f - 1)
                    elif f == 0:
                        pe.wait_ge(modulation2_ready, 1)
                    tile = slice(f * D, (f + 1) * D)
                    pe.matmul(p_h[f % 2][:, :], w1_lo[:, tile], hi, start=True, stop=False)
                    pe.matmul(p_h[f % 2][:, :], w1_hi[:, tile], lo, start=False, stop=False)
                    pe.matmul(p_h[f % 2][:, :], w1_hi[:, tile], hi, start=False, stop=True).then_inc(w1_done, 1)
                return stage

            def ff_bias(c):
                if c == 0:
                    pe.wait_ge(b2_ready, 1)
                elif c == 1:
                    pe.wait_ge(c_part_ready, 1)
                else:
                    pe.wait_ge(gated_ff_ready, c - 1)
                pe.matmul(p_y[c % 2][:, :], ones[:, :], b2_parts[:, :], start=True, stop=False)

            def feed_forward(f, js):
                def stage(c):
                    if js[0] == 0:
                        if c == 0 and f == 0:
                            pe.wait_ge(w2_landed, 16)
                        pe.wait_ge(h_ready, NF * c + f + 1)
                    for j in js:
                        last = pe.matmul(p_y[c % 2][:, j * D:(j + 1) * D], h[:, c % 2, f, j * NB:(j + 1) * NB],
                                         w2_sb[:, f, :], start=False, stop=(f == NF - 1 and j == STEPS - 1))
                    if f == NF - 1 and js[-1] == STEPS - 1:
                        last.then_inc(w2_done, 1)
                return stage

            pe.wait_ge(ident_ready, 1)
            pe.wait_ge(cond_landed, 16)
            turn(p_b[:, 0:NB], cond_sb[:, :], NB).then_inc(condT_in_psum, 1)
            pe.wait_ge(condT_ready, 1)
            pe.wait_ge(wmod_a_landed, 16)
            pe.wait_ge(ones_ready, 1)
            modulation(p_y[0][:, 0:2 * D], 0, 2 * D, bm_landed).then_inc(mod_a_in_psum, 1)
            pe.wait_ge(wmod_landed, 16)
            modulation(p_h[0][:, 0:2 * D], 2 * D, 2 * D, bm_landed)
            pe.wait_ge(d_landed, 16)
            pe.matmul(p_h[0][:, 2 * D:3 * D], ones_row[:, :], d_row[:, :], start=True, stop=True) \
              .then_inc(mod_b_in_psum, 1)
            pe.wait_ge(wc_landed, 16)
            modulation(p_h[1][:, :], 4 * D, 4 * D, bc_landed).then_inc(mod_c_in_psum, 1)
            pe.wait_ge(c_landed, 32)
            turn(p_y[1][:, 0:D], c_parts[:, 0:4, :].rearrange("d g p -> d (g p)"), D)
            turn(p_y[1][:, D:2 * D], c_parts[:, 1:5, :].rearrange("d g p -> d (g p)"), D)
            pe.wait_ge(b1_landed, 16)
            turn(p_y[1][:, 2 * D:2 * D + NF], b1_rows[:, :], NF).then_inc(cT_in_psum, 1)
            turn_u(0)
            pe.wait_ge(b_landed, 32)
            pe.wait_ge(turns_ready, 1)
            pe.matmul(p_t2[:, 0:STEPS * R], b_parts[:, :], factors[0:R, 0:STEPS, :].rearrange("p s r -> p (s r)"),
                      start=True, stop=True).then_inc(bT_in_psum, 1)
            state_inputs(0)

            def turn_u_rest(c):
                if c >= 1:
                    turn_u(c)

            def state_inputs_rest(c):
                if c >= 1:
                    state_inputs(c)

            hidden0, hidden1, hidden2, hidden3 = (hidden(f) for f in range(NF))
            ff0, ff1, ff2, ff3 = (feed_forward(f, range(STEPS)) for f in range(NF))
            run([(ff3, 0), (hidden1, 1), (hidden2, 1), (state_outputs, 3), (ff0, 1), (ff_bias, 2), (ff1, 1),
                 (turn_u_rest, 4), (turn_w, 2), (hidden3, 1), (state_inputs_rest, 4), (ff2, 1), (hidden0, 2)])


_INS = ['x', 'cond_1024', 'L0_cond_Wm', 'L0_cond_bm', 'L0_cond_Lam_re', 'L0_cond_Lam_im', 'L0_cond_B_re',
        'L0_cond_B_im', 'L0_cond_C_re', 'L0_cond_C_im', 'L0_cond_D_diag', 'L0_cond_log_step', 'L0_cond_Wc',
        'L0_cond_bc', 'L0_cond_W1', 'L0_cond_b1', 'L0_cond_W2', 'L0_cond_b2']
_OUTS = [((128, 32, 128), 'float32')]


def kernel(**inputs):
    import numpy as _np
    import concourse.bacc as _bacc
    from concourse import mybir as _mybir
    from concourse.bass_utils import run_bass_kernel_spmd as _run

    nc = _bacc.Bacc("TRN2", target_bir_lowering=False, num_devices=1)
    arrays, args = {}, []
    for name in _INS:
        a = _np.ascontiguousarray(inputs[name])
        arrays[f"in_{name}_dram"] = a
        args.append(nc.dram_tensor(f"in_{name}_dram", a.shape, _mybir.dt.from_np(a.dtype), kind="ExternalInput").ap())
    for i, (shape, dtype) in enumerate(_OUTS):
        dt = _mybir.dt.from_np(_np.dtype(dtype))
        args.append(nc.dram_tensor(f"out_{i}_dram", shape, dt, kind="ExternalOutput").ap())
    conditioned_s5_block(nc, *args)
    r = _run(nc, [arrays], core_ids=[0])
    return r.results[0]["out_0_dram"]
```

```python
from contextlib import ExitStack

import numpy as np

import concourse.bass as bass
from concourse import mybir

ALU = mybir.AluOpType
ACT = mybir.ActivationFunctionType
F32 = mybir.dt.float32
F32R = mybir.dt.float32r
I32 = mybir.dt.int32

STEPS = 4
LAST_PARTS = slice(0, STEPS // 2), slice(STEPS // 2, STEPS)
RING = 3
PSUM_COLUMNS = 512

SERIES = [1.0, 1 / 2, 1 / 6, 1 / 24, 1 / 120, 1 / 720, 1 / 5040, 1 / 40320]
ROUND = 1.5 * 2.0 ** 23
LOG2E = float(np.log2(np.e))
LN2_HI = 0.693359375
LN2_LO = float(np.log(2.0) - LN2_HI)
TWO_PI_HI = 6.28125
TWO_PI_MID = float(np.float32(2 * np.pi - TWO_PI_HI))
TWO_PI_LO = float(2 * np.pi - TWO_PI_HI - TWO_PI_MID)
PI_BELOW = 3.1415925
EXP_FLOOR = -87.0
LN_EPS = 1e-5


def conditioned_s5_block(nc, x, cond, Wm, bm, Lam_re, Lam_im, B_re, B_im, C_re, C_im, D_diag,
                         log_step, Wc, bc, W1, b1, W2, b2, out):
    NB, L, D = x.shape
    P = Lam_re.shape[0]
    FF = W1.shape[1]
    NC = L // STEPS
    NF = FF // D
    CW = STEPS * D
    HB = NB // 2
    R = 2 * P
    assert NB == D == 128 and P == 32 and CW == PSUM_COLUMNS and NF * D == FF

    with ExitStack() as ctx:
        def sb(name, shape, dt=F32):
            return ctx.enter_context(nc.sbuf_tensor(name, shape, dt))

        def bank(name):
            return ctx.enter_context(nc.psum_tensor(name, [128, PSUM_COLUMNS], F32))

        def sem(name):
            return ctx.enter_context(nc.semaphore(name))

        cond_sb = sb("cond_sb", [NB, D])
        condT = sb("condT", [D, NB])
        wmod = sb("wmod", [D, 8 * D])
        mod_bias = sb("mod_bias", [1, 8 * D])
        free_rows = sb("free_rows", [1, 2 * D])
        ones_row = sb("ones_row", [1, 128])
        ident = sb("ident", [128, 128])
        same_part = sb("same_part", [128, R])
        other_part = sb("other_part", [128, R])
        b1_rows = sb("b1_rows", [NF, D])
        b1_col = sb("b1_col", [D, NF])
        w1_sb = sb("w1_sb", [D, FF])
        w1_hi = sb("w1_hi", [D, FF], F32R)
        w1_lo = sb("w1_lo", [D, FF], F32R)
        w2_sb = sb("w2_sb", [D, NF, D])
        scale1 = sb("scale1", [NB, D])
        shift1 = sb("shift1", [NB, D])
        scale_ff = sb("scale_ff", [NB, D])
        scale2 = sb("scale2", [NB, D])
        shift2a = sb("shift2a", [NB, D])
        shift2 = sb("shift2", [NB, D])
        gate_a = sb("gate_a", [NB, D])
        gate_d = sb("gate_d", [NB, D])
        gate_ff = sb("gate_ff", [NB, D])
        gate_b2 = sb("gate_b2", [NB, D])

        lam = sb("lam", [128, 3])
        series_even = sb("series_even", [128, 4])
        series_odd = sb("series_odd", [128, 4])
        step_no = sb("step_no", [128, STEPS + 1])
        sign = sb("sign", [128, 1])
        small = sb("small", [128, 160])
        first_sine = sb("first_sine", [1, 1])
        first_gelu = sb("first_gelu", [1, 1])
        angles = sb("angles", [128, 2, STEPS + 1])
        sines = sb("sines", [128, 2, STEPS + 1])
        b_parts = sb("b_parts", [R, D])
        factor_part = sb("factor_part", [128, STEPS + 1, R])
        factor_part2 = sb("factor_part2", [128, STEPS + 1, R])
        factors = sb("factors", [128, STEPS + 1, R])
        bT = sb("bT", [D, STEPS, R])
        c_parts = sb("c_parts", [D, 5, P])
        cT = sb("cT", [128, 2, D])
        c_im = sb("c_im", [128, STEPS + 1])
        c_part = sb("c_part", [128, STEPS, D])
        c_turned = sb("c_turned", [128, STEPS, D])

        x_sb = sb("x_sb", [NB, NC, CW])
        n1 = sb("n1", [NB, RING, CW])
        u_part = sb("u_part", [NB, RING, CW])
        u = sb("u", [NB, RING, CW])
        uT = sb("uT", [D, RING, CW])
        z = sb("z", [128, NC, STEPS, HB])
        skip_part = sb("skip_part", [NB, RING, CW])
        skip = sb("skip", [NB, RING, CW])
        gated = sb("gated", [NB, RING, CW])
        y1 = sb("y1", [NB, NC, CW])
        y1b = sb("y1b", [NB, RING, CW])
        n2 = sb("n2", [NB, RING, CW])
        w_part = sb("w_part", [NB, RING, CW])
        w = sb("w", [NB, RING, CW])
        v_hi = sb("v_hi", [D, RING, CW], F32R)
        v_lo = sb("v_lo", [D, RING, CW], F32R)
        h = sb("h", [D, 2, NF, CW])
        gated_ff = sb("gated_ff", [NB, RING, CW])
        y2 = sb("y2", [NB, NC, CW])
        raw_stats = [sb(f"raw_stats{k}", [NB, NC, STEPS, 6]) for k in (1, 2)]
        mean_var = [sb(f"mean_var{k}", [NB, NC, STEPS, 2]) for k in (1, 2)]
        var_eps = [sb(f"var_eps{k}", [NB, NC, STEPS]) for k in (1, 2)]
        neg_mean = [sb(f"neg_mean{k}", [NB, NC, STEPS]) for k in (1, 2)]
        rstd = [sb(f"rstd{k}", [NB, NC, STEPS]) for k in (1, 2)]
        norm_bias = [sb(f"norm_bias{k}", [NB, NC, STEPS]) for k in (1, 2)]

        minus_half = sb("minus_half", [NB, STEPS])

        p_t1, p_t2, p_b, p_c = bank("p_t1"), bank("p_t2"), bank("p_b"), bank("p_c")
        p_h = [bank("p_h0"), bank("p_h1")]
        p_y = [bank("p_y0"), bank("p_y1")]

        x_landed = [sem(f"x_landed{c}") for c in range(NC)]
        log_step_landed, lam_landed, b_landed, c_landed = (sem("log_step_landed"), sem("lam_landed"), sem("b_landed"),
                                                           sem("c_landed"))
        cond_landed, wmod_a_landed, wmod_landed = sem("cond_landed"), sem("wmod_a_landed"), sem("wmod_landed")
        wc_landed, bm_landed, bc_landed, free_rows_landed = (sem("wc_landed"), sem("bm_landed"), sem("bc_landed"),
                                                             sem("free_rows_landed"))
        w1_landed, w2_landed, b1_landed = sem("w1_landed"), sem("w2_landed"), sem("b1_landed")
        const_chain, ident_ready, const_ready = sem("const_chain"), sem("ident_ready"), sem("const_ready")
        ones_ready = sem("ones_ready")
        chain = sem("chain")
        angles_ready, sines_ready = sem("angles_ready"), sem("sines_ready")
        turns_ready, bT_in_psum, bT_ready = sem("turns_ready"), sem("bT_in_psum"), sem("bT_ready")
        cT_in_psum, cT_ready, b1_col_ready = sem("cT_in_psum"), sem("cT_ready"), sem("b1_col_ready")
        c_im_ready, c_part_ready, c_turned_ready = sem("c_im_ready"), sem("c_part_ready"), sem("c_turned_ready")
        condT_in_psum, condT_ready = sem("condT_in_psum"), sem("condT_ready")
        mod_a_in_psum, mod_b_in_psum = sem("mod_a_in_psum"), sem("mod_b_in_psum")
        mod_c_in_psum = sem("mod_c_in_psum")
        modulation1_ready, gates_ready, modulation2_ready = (sem("modulation1_ready"), sem("gates_ready"),
                                                             sem("modulation2_ready"))
        ff_tables_ready = sem("ff_tables_ready")
        w1_hi_ready, w1_split = sem("w1_hi_ready"), sem("w1_split")
        raw_ready, stats_ready = [sem("raw1_ready"), sem("raw2_ready")], [sem("stats1_ready"), sem("stats2_ready")]
        var_eps_ready = [sem("var_eps1_ready"), sem("var_eps2_ready")]
        power_ready = [sem("power1_ready"), sem("power2_ready")]
        rstd_ready = [sem("rstd1_ready"), sem("rstd2_ready")]
        n_ready = [sem("n1_ready"), sem("n2_ready")]
        u_part_ready, u_ready = sem("u_part_ready"), sem("u_ready")
        u_in_psum, uT_ready = sem("u_in_psum"), sem("uT_ready")
        b_done, z_ready = sem("b_done"), sem("z_ready")
        c_done = sem("c_done")
        skip_part_ready, skip_ready = sem("skip_part_ready"), sem("skip_ready")
        gated_ready, y1_ready, y1b_ready = sem("gated_ready"), sem("y1_ready"), sem("y1b_ready")
        w_part_ready, w_ready, w_in_psum = sem("w_part_ready"), sem("w_ready"), sem("w_in_psum")
        v_hi_ready, v_lo_ready = sem("v_hi_ready"), sem("v_lo_ready")
        w1_done, h_ready, w2_done = sem("w1_done"), sem("h_ready"), sem("w2_done")
        gated_ff_ready, y2_ready, stored = sem("gated_ff_ready"), sem("y2_ready"), sem("stored")

        def over_steps(table):
            return table[:, :].unsqueeze(1).to_broadcast([128, STEPS, 128])

        def steps(ap):
            return ap.rearrange("p (s d) -> p s d", s=STEPS)

        def run(stages):
            for turn_no in range(min(first - ahead for _, ahead, first in stages), NC):
                for stage, ahead, first in stages:
                    if first <= turn_no + ahead < NC:
                        stage(turn_no + ahead)

        block = ctx.enter_context(nc.Block())

        @block.sync
        def _(sp):
            def load_x(c):
                sp.dma_start(x_sb[:, c, :], x[:, c * STEPS:(c + 1) * STEPS, :].rearrange("b s d -> b (s d)")) \
                  .then_inc(x_landed[c], 16)

            def load_lam(source, k, landed):
                sp.dma_start(lam[:, k:k + 1], source.rearrange("(g p o) -> g p o", g=1, o=1)
                             .broadcast_to([4, P, 1])).then_inc(landed, 16)

            load_lam(log_step, 2, log_step_landed)
            load_x(0)
            load_lam(Lam_im, 1, lam_landed)
            load_lam(Lam_re, 0, lam_landed)
            sp.dma_start(mod_bias[:, 0:6 * D], bm.rearrange("(o n) -> o n", o=1)).then_inc(bm_landed, 16)
            sp.dma_start(wmod[:, 2 * D:6 * D], Wm[:, 2 * D:6 * D]).then_inc(wmod_landed, 16)
            sp.dma_start(wmod[:, 6 * D:8 * D], Wc).then_inc(wc_landed, 16)
            sp.dma_start(b_parts[0:P, :], B_re).then_inc(b_landed, 16)
            sp.dma_start(b_parts[P:R, :], B_im).then_inc(b_landed, 16)
            sp.dma_start(c_parts[:, 0::2, :], C_re.rearrange("d (o p) -> d o p", o=1).broadcast_to([D, 3, P])) \
              .then_inc(c_landed, 16)
            sp.dma_start(c_parts[:, 1::2, :], C_im.rearrange("d (o p) -> d o p", o=1).broadcast_to([D, 2, P])) \
              .then_inc(c_landed, 16)
            load_x(1)
            sp.dma_start(w1_sb[:, :], W1).then_inc(w1_landed, 16)
            load_x(2)
            sp.dma_start(w2_sb[:, :, :], W2.rearrange("(f k) d -> k f d", k=D)).then_inc(w2_landed, 16)
            for c in range(3, NC):
                load_x(c)
            for c in range(NC - 1):
                sp.wait_ge(y2_ready, c + 1)
                sp.dma_start(out[:, c * STEPS:(c + 1) * STEPS, :].rearrange("b s d -> b (s d)"), y2[:, c, :]) \
                  .then_inc(stored, 16)
            for k, part in enumerate(LAST_PARTS):
                sp.wait_ge(y2_ready, NC + k)
                at = slice((NC - 1) * STEPS + part.start, (NC - 1) * STEPS + part.stop)
                sp.dma_start(out[:, at, :].rearrange("b s d -> b (s d)"),
                             y2[:, NC - 1, part.start * D:part.stop * D]).then_inc(stored, 16)
            sp.wait_ge(stored, 16 * (NC + 1))

        @block.gpsimd
        def _(pool):
            count = {"const": 0}

            def const_link(ins):
                count["const"] += 1
                ins.then_inc(const_chain, 1)
                pool.wait_ge(const_chain, count["const"])

            def mark(table, offsets):
                for at in offsets:
                    ins = pool.affine_select(out=table[:, :], in_=table[:, :], compare_op=ALU.not_equal, fill=1.0,
                                             base=-at, pattern=[[-1, table.shape[1]]], channel_multiplier=1)
                    if at != offsets[-1]:
                        const_link(ins)
                return ins

            def rstd_of(k, c):
                pool.wait_ge(stats_ready[k], c + 1)
                pool.tensor_scalar(var_eps[k][:, c, :], mean_var[k][:, c, :, 1], LN_EPS, None, ALU.add) \
                    .then_inc(var_eps_ready[k], 1)
                pool.tensor_scalar(neg_mean[k][:, c, :], mean_var[k][:, c, :, 0], -1.0, None, ALU.mult)
                pool.wait_ge(var_eps_ready[k], c + 1)
                pool.tensor_tensor(rstd[k][:, c, :], var_eps[k][:, c, :], minus_half[:, :], ALU.pow) \
                    .then_inc(power_ready[k], 1)
                pool.wait_ge(power_ready[k], c + 1)
                pool.tensor_tensor(norm_bias[k][:, c, :], neg_mean[k][:, c, :], rstd[k][:, c, :], ALU.mult) \
                    .then_inc(rstd_ready[k], 1)

            def scale_u(c):
                s = c % RING
                if c == 0:
                    pool.wait_ge(modulation1_ready, 1)
                if c >= RING:
                    pool.wait_ge(u_ready, c - RING + 1)
                pool.wait_ge(n_ready[0], c + 1)
                pool.tensor_tensor(steps(u_part[:, s, :]), steps(n1[:, s, :]), over_steps(scale1), ALU.mult) \
                    .then_inc(u_part_ready, 1)

            def shift_u(c):
                s = c % RING
                if c >= RING:
                    pool.wait_ge(u_in_psum, c - RING + 1)
                    pool.wait_ge(skip_part_ready, c - RING + 1)
                pool.wait_ge(u_part_ready, c + 1)
                pool.tensor_tensor(steps(u[:, s, :]), steps(u_part[:, s, :]), over_steps(shift1), ALU.add) \
                    .then_inc(u_ready, 1)

            def scale_skip(c):
                s = c % RING
                if c == 0:
                    pool.wait_ge(gates_ready, 1)
                if c >= RING:
                    pool.wait_ge(skip_ready, c - RING + 1)
                pool.wait_ge(u_ready, c + 1)
                pool.tensor_tensor(steps(skip_part[:, s, :]), steps(u[:, s, :]), over_steps(gate_d), ALU.mult) \
                    .then_inc(skip_part_ready, 1)

            def add_skip(c):
                s = c % RING
                if c >= RING:
                    pool.wait_ge(y1_ready, c - RING + 1)
                pool.wait_ge(skip_part_ready, c + 1)
                pool.tensor_tensor(skip[:, s, :], skip_part[:, s, :], x_sb[:, c, :], ALU.add).then_inc(skip_ready, 1)

            const_link(pool.memset(ident[:, :], 0.0))
            mark(ident, [0]).then_inc(ident_ready, 1)
            pool.memset(minus_half[:, :], -0.5)
            pool.memset(same_part[:, :], 0.0)
            const_link(pool.memset(other_part[:, :], 0.0))
            mark(same_part, [0, R]).then_inc(const_ready, 1)
            mark(other_part, [-P, P, 3 * P]).then_inc(const_ready, 1)
            pool.dma_start(free_rows[:, 0:D], D_diag.rearrange("(o n) -> o n", o=1)).then_inc(free_rows_landed, 16)
            pool.dma_start(free_rows[:, D:2 * D], b2.rearrange("(o n) -> o n", o=1)).then_inc(free_rows_landed, 16)
            pool.dma_start(mod_bias[:, 6 * D:8 * D], bc.rearrange("(o n) -> o n", o=1)).then_inc(bc_landed, 16)
            pool.dma_start(b1_rows[:, :], b1.rearrange("(f d) -> f d", f=NF)).then_inc(b1_landed, 16)
            rstd_of(0, 0)
            scale_u(0)
            shift_u(0)
            rstd_of(0, 1)
            scale_skip(0)
            add_skip(0)

            def rstd1(c):
                rstd_of(0, c)

            def rstd2(c):
                rstd_of(1, c)

            scale_u(1)
            shift_u(1)
            scale_skip(1)
            add_skip(1)
            run([(scale_skip, 1, 2), (rstd2, 0, 0), (scale_u, 2, 2), (shift_u, 2, 2), (add_skip, 1, 2),
                 (rstd1, 3, 2)])

        @block.vector
        def _(dve):
            count = {"chain": 0}

            def note(ins):
                count["chain"] += 1
                return ins.then_inc(chain, 1)

            def link(ins):
                note(ins)
                dve.wait_ge(chain, count["chain"])

            cells = iter(range(160))

            def cell(width=1):
                at = [next(cells) for _ in range(width)]
                return small[:, at[0]:at[-1] + 1]

            def raw_stats_of(k, c, js=range(STEPS)):
                if js[0] == 0:
                    if k == 0:
                        dve.wait_ge(x_landed[c], 16)
                    else:
                        dve.wait_ge(y1_ready, c + 1)
                src = x_sb if k == 0 else y1
                for j in js:
                    ins = dve.bn_stats(raw_stats[k][:, c, j, :], src[:, c, j * D:(j + 1) * D])
                if js[-1] == STEPS - 1:
                    ins.then_inc(raw_ready[k], 1)

            def mean_var_of(k, c):
                dve.wait_ge(raw_ready[k], c + 1)
                for j in range(STEPS):
                    ins = dve.bn_aggr(mean_var[k][:, c, j, :], raw_stats[k][:, c, j, :])
                ins.then_inc(stats_ready[k], 1)

            dve.memset(ones_row[:, :], 1.0).then_inc(ones_ready, 1)
            for k in range(4):
                dve.memset(series_even[:, k:k + 1], SERIES[2 * k])
                dve.memset(series_odd[:, k:k + 1], SERIES[2 * k + 1])
            for j in range(STEPS + 1):
                dve.memset(step_no[:, j:j + 1], float(j))
            link(dve.memset(sign[:, :], 1.0))
            dve.memset(sign[0:P, :], -1.0)
            note(dve.memset(sign[2 * P:3 * P, :], -1.0))

            lam_re, lam_im, log_dt = (lam[:, k:k + 1] for k in range(3))
            W = STEPS + 1

            clamped, shifted, whole, f1, f, power = (cell() for _ in range(6))
            f2, f4, s4, s2, s1, f_power = cell(), cell(), cell(4), cell(2), cell(), cell()
            dve.wait_ge(log_step_landed, 16)
            note(dve.tensor_scalar(shifted, log_dt, LOG2E, ROUND, ALU.mult, ALU.add))
            link(dve.tensor_scalar(clamped, log_dt, EXP_FLOOR, None, ALU.max))
            link(dve.tensor_scalar(whole, shifted, ROUND, -126.0, ALU.subtract, ALU.max))
            link(dve.scalar_tensor_tensor(f1, whole, -LN2_HI, clamped, ALU.mult, ALU.add))
            note(dve.scalar_tensor_tensor(f, whole, -LN2_LO, f1, ALU.mult, ALU.add))
            link(dve.tensor_scalar(power.bitcast(I32), whole, 127.0, 2.0 ** 23, ALU.add, ALU.mult))
            note(dve.tensor_tensor(f2, f, f, ALU.mult))
            note(dve.scalar_tensor_tensor(s4, series_odd[:, :], f, series_even[:, :], ALU.mult, ALU.add))
            dve.wait_ge(chain, count["chain"])
            note(dve.scalar_tensor_tensor(s2, s4[:, 1::2], f2, s4[:, 0::2], ALU.mult, ALU.add))
            note(dve.tensor_tensor(f4, f2, f2, ALU.mult))
            note(dve.tensor_tensor(f_power, f, power, ALU.mult))
            raw_stats_of(0, 0, [0])
            dve.wait_ge(chain, count["chain"])
            note(dve.scalar_tensor_tensor(s1, s2[:, 1:2], f4, s2[:, 0:1], ALU.mult, ALU.add))
            dt, theta, decay_log, sq_im, norm2, inv_norm2 = (cell() for _ in range(6))
            raw_stats_of(0, 0, [1])
            dve.wait_ge(chain, count["chain"])
            note(dve.scalar_tensor_tensor(dt, s1, f_power, power, ALU.mult, ALU.add))
            raw_stats_of(0, 0, [2])
            dve.wait_ge(chain, count["chain"])
            dve.wait_ge(lam_landed, 32)
            note(dve.tensor_tensor(theta, lam_im, dt, ALU.mult))
            note(dve.tensor_tensor(sq_im, lam_im, lam_im, ALU.mult))
            note(dve.tensor_scalar(decay_log, lam_re, dt, EXP_FLOOR, ALU.mult, ALU.max))
            raw_stats_of(0, 0, [3])
            mean_var_of(0, 0)
            dve.wait_ge(chain, count["chain"])

            angle, rounds_s, rounds, a1, a2, a3 = (cell(W) for _ in range(6))
            shifted, whole, f1, f, power, power_m1 = (cell() for _ in range(6))
            f2, f4, s4, s2, s1, f_power = cell(), cell(), cell(4), cell(2), cell(), cell()
            decay, decay_m1, ratio_re, ratio_im = (cell() for _ in range(4))
            note(dve.tensor_scalar(angle, step_no[:, :], theta, None, ALU.mult))
            note(dve.tensor_scalar(shifted, decay_log, LOG2E, ROUND, ALU.mult, ALU.add))
            link(dve.scalar_tensor_tensor(norm2, lam_re, lam_re, sq_im, ALU.mult, ALU.add))
            link(dve.tensor_scalar(rounds_s, angle, float(1 / (2 * np.pi)), ROUND, ALU.mult, ALU.add))
            note(dve.tensor_scalar(rounds, rounds_s, ROUND, None, ALU.subtract))
            link(dve.tensor_scalar(whole, shifted, ROUND, None, ALU.subtract))
            note(dve.scalar_tensor_tensor(a1, rounds, -TWO_PI_HI, angle, ALU.mult, ALU.add))
            link(dve.scalar_tensor_tensor(f1, whole, -LN2_HI, decay_log, ALU.mult, ALU.add))
            note(dve.scalar_tensor_tensor(a2, rounds, -TWO_PI_MID, a1, ALU.mult, ALU.add))
            link(dve.scalar_tensor_tensor(f, whole, -LN2_LO, f1, ALU.mult, ALU.add))
            note(dve.scalar_tensor_tensor(a3, rounds, -TWO_PI_LO, a2, ALU.mult, ALU.add))
            link(dve.tensor_scalar(power.bitcast(I32), whole, 127.0, 2.0 ** 23, ALU.add, ALU.mult))
            note(dve.tensor_scalar(angles[:, 0, :], a3, -PI_BELOW, PI_BELOW, ALU.max, ALU.min))
            note(dve.scalar_tensor_tensor(s4, series_odd[:, :], f, series_even[:, :], ALU.mult, ALU.add))
            link(dve.tensor_tensor(f2, f, f, ALU.mult))
            dve.tensor_scalar(angles[:, 1, :], angles[:, 0, :], 0.5, None, ALU.mult).then_inc(angles_ready, 1)
            note(dve.tensor_tensor(f4, f2, f2, ALU.mult))
            note(dve.scalar_tensor_tensor(s2, s4[:, 1::2], f2, s4[:, 0::2], ALU.mult, ALU.add))
            note(dve.tensor_tensor(f_power, f, power, ALU.mult))
            note(dve.tensor_scalar(power_m1, power, -1.0, None, ALU.add))
            link(dve.reciprocal(inv_norm2, norm2))
            sin, sin_half = sines[:, 0, :], sines[:, 1, :]
            half_sq, cos, minus_sin, sign_cos, sign_sin, w_re_a, w_im_a = (cell(W) for _ in range(7))
            c_re = cell(W)
            w_re, w_im = cell(W), cell(W)
            cos_m1, num_re, sin_re, sin_im, t1, t2, q_re, minus_q_im = (cell() for _ in range(8))
            note(dve.scalar_tensor_tensor(s1, s2[:, 1:2], f4, s2[:, 0:1], ALU.mult, ALU.add))
            note(dve.tensor_tensor(ratio_re, lam_re, inv_norm2, ALU.mult))
            note(dve.tensor_tensor(ratio_im, lam_im, inv_norm2, ALU.mult))
            dve.wait_ge(sines_ready, 1)
            link(dve.tensor_tensor(half_sq, sin_half, sin_half, ALU.mult))
            note(dve.tensor_scalar(cos, half_sq, -2.0, 1.0, ALU.mult, ALU.add))
            note(dve.tensor_scalar(cos_m1, half_sq[:, 1:2], -2.0, None, ALU.mult))
            note(dve.scalar_tensor_tensor(decay, s1, f_power, power, ALU.mult, ALU.add))
            note(dve.scalar_tensor_tensor(decay_m1, s1, f_power, power_m1, ALU.mult, ALU.add))
            note(dve.tensor_tensor(sin_im, sin[:, 1:2], ratio_im, ALU.mult))
            note(dve.tensor_tensor(sin_re, sin[:, 1:2], ratio_re, ALU.mult))
            note(dve.tensor_scalar(sign_sin, sin, sign[:, 0:1], None, ALU.mult))
            note(dve.tensor_scalar(minus_sin, sin, -1.0, None, ALU.mult))
            dve.tensor_scalar(c_im[:, :], sin, -2.0, None, ALU.mult).then_inc(c_im_ready, 1)
            dve.wait_ge(chain, count["chain"])
            note(dve.scalar_tensor_tensor(num_re, decay_m1, cos[:, 1:2], cos_m1, ALU.mult, ALU.add))
            note(dve.tensor_tensor(t1, decay, sin_im, ALU.mult))
            note(dve.tensor_tensor(t2, decay, sin_re, ALU.mult))
            raw_stats_of(0, 1, [0])
            dve.wait_ge(chain, count["chain"])
            note(dve.scalar_tensor_tensor(q_re, num_re, ratio_re, t1, ALU.mult, ALU.add))
            note(dve.scalar_tensor_tensor(minus_q_im, num_re, ratio_im, t2, ALU.mult, ALU.subtract))
            note(dve.tensor_scalar(sign_cos, cos, sign[:, 0:1], None, ALU.mult))
            raw_stats_of(0, 1, [1])
            dve.wait_ge(chain, count["chain"])
            note(dve.tensor_scalar(w_re_a[:, 0:STEPS], cos[:, 0:STEPS], q_re, None, ALU.mult))
            note(dve.tensor_scalar(w_im_a[:, 0:STEPS], sign_sin[:, 0:STEPS], q_re, None, ALU.mult))
            raw_stats_of(0, 1, [2])
            dve.wait_ge(chain, count["chain"])
            note(dve.scalar_tensor_tensor(w_im[:, 0:STEPS], sign_cos[:, 0:STEPS], minus_q_im, w_im_a[:, 0:STEPS],
                                          ALU.mult, ALU.add))
            note(dve.scalar_tensor_tensor(w_re[:, 0:STEPS], minus_sin[:, 0:STEPS], minus_q_im, w_re_a[:, 0:STEPS],
                                          ALU.mult, ALU.add))
            note(dve.tensor_tensor(w_re[:, STEPS:W], decay, cos[:, STEPS:W], ALU.mult))
            note(dve.scalar_tensor_tensor(w_im[:, STEPS:W], sign_sin[:, STEPS:W], -1.0, decay, ALU.mult, ALU.mult))
            raw_stats_of(0, 1, [3])
            dve.wait_ge(chain, count["chain"])
            def factor_matrices(first, last):
                by_row = [128, last - first, R]
                note(dve.tensor_tensor(factor_part[:, first:last, :], same_part[:, :].unsqueeze(1).to_broadcast(by_row),
                                       w_re[:, first:last].unsqueeze(2).to_broadcast(by_row), ALU.mult))
                note(dve.tensor_tensor(factor_part2[:, first:last, :],
                                       other_part[:, :].unsqueeze(1).to_broadcast(by_row),
                                       w_im[:, first:last].unsqueeze(2).to_broadcast(by_row), ALU.mult))

            dve.wait_ge(const_ready, 2)
            factor_matrices(0, STEPS)
            mean_var_of(0, 1)
            dve.wait_ge(chain, count["chain"])
            dve.tensor_tensor(factors[:, 0:STEPS, :], factor_part[:, 0:STEPS, :], factor_part2[:, 0:STEPS, :],
                              ALU.add).then_inc(turns_ready, 1)
            note(dve.tensor_scalar(c_re, sign_cos, -2.0, None, ALU.mult))

            def turn_c(j):
                dve.wait_ge(c_part_ready, 1)
                dve.scalar_tensor_tensor(c_turned[:, j, :], cT[:, 0, :], c_re[:, j:j + 1], c_part[:, j, :],
                                         ALU.mult, ALU.add).then_inc(c_turned_ready, 1)

            def copy_bT():
                dve.wait_ge(bT_in_psum, 1)
                dve.tensor_copy(bT[:, :, :], p_t2[:, 0:STEPS * R].rearrange("p (s r) -> p s r", s=STEPS)) \
                   .then_inc(bT_ready, 1)

            def second_modulation():
                dve.wait_ge(ff_tables_ready, 1)
                note(dve.scalar_tensor_tensor(scale2[:, :], p_h[1][:, 2 * D:3 * D], 1.0, scale_ff[:, :],
                                              ALU.add, ALU.mult))
                link(dve.tensor_tensor(shift2a[:, :], p_h[1][:, 3 * D:4 * D], scale_ff[:, :], ALU.mult))
                note(dve.tensor_tensor(gate_b2[:, :], gate_ff[:, :], p_h[0][:, 3 * D:4 * D], ALU.mult))
                dve.tensor_tensor(shift2[:, :], p_h[0][:, D:2 * D], shift2a[:, :], ALU.add) \
                   .then_inc(modulation2_ready, 1)

            def low_w1(f):
                tile = slice(f * D, (f + 1) * D)
                if f == 0:
                    dve.wait_ge(w1_hi_ready, 1)
                dve.tensor_tensor(w1_lo[:, tile], w1_sb[:, tile], w1_hi[:, tile].bitcast(F32), ALU.subtract) \
                   .then_inc(w1_split, 1)

            def recur(j):
                def stage(c):
                    if j == 0:
                        dve.wait_ge(b_done, c + 1)
                        ins = dve.tensor_copy(z[:, c, 0, :], p_b[:, 0:HB])
                    else:
                        dve.wait_ge(z_ready, STEPS * c + j)
                        ins = dve.scalar_tensor_tensor(z[:, c, j, :], z[:, c, j - 1, :], decay,
                                                       p_b[:, j * HB:(j + 1) * HB], ALU.mult, ALU.add)
                    ins.then_inc(z_ready, 1)
                return stage

            def gate_state(c):
                s = c % RING
                dve.wait_ge(c_done, c + 1)
                if c >= RING:
                    dve.wait_ge(y1_ready, c - RING + 1)
                dve.tensor_tensor(steps(gated[:, s, :]), steps(p_c[:, :]), over_steps(gate_a), ALU.mult) \
                   .then_inc(gated_ready, 1)

            def add_state(c):
                dve.wait_ge(skip_ready, c + 1)
                dve.wait_ge(gated_ready, c + 1)
                dve.tensor_tensor(y1[:, c, :], gated[:, c % RING, :], skip[:, c % RING, :], ALU.add) \
                   .then_inc(y1_ready, 1)

            def scale_w(c):
                s = c % RING
                dve.wait_ge(n_ready[1], c)
                if c >= RING:
                    dve.wait_ge(w_ready, c - RING + 1)
                dve.tensor_tensor(steps(w_part[:, s, :]), steps(n2[:, s, :]), over_steps(scale2), ALU.mult) \
                   .then_inc(w_part_ready, 1)

            def shift_w(c):
                s = c % RING
                if c >= RING:
                    dve.wait_ge(w_in_psum, c - RING + 1)
                dve.wait_ge(w_part_ready, c + 1)
                dve.tensor_tensor(steps(w[:, s, :]), steps(w_part[:, s, :]), over_steps(shift2), ALU.add) \
                   .then_inc(w_ready, 1)

            def scale_first_w():
                dve.wait_ge(modulation2_ready, 1)
                dve.wait_ge(stats_ready[1], 1)
                for j in range(STEPS):
                    at = slice(j * D, (j + 1) * D)
                    ins = dve.scalar_tensor_tensor(w_part[:, 0, at], y1[:, 0, at], mean_var[1][:, 0, j, 0:1],
                                                   scale2[:, :], ALU.subtract, ALU.mult)
                ins.then_inc(w_part_ready, 1)

            def shift_first_w():
                dve.wait_ge(w_part_ready, 1)
                dve.wait_ge(power_ready[1], 1)
                for j in range(STEPS):
                    at = slice(j * D, (j + 1) * D)
                    ins = dve.scalar_tensor_tensor(w[:, 0, at], w_part[:, 0, at], rstd[1][:, 0, j:j + 1],
                                                   shift2[:, :], ALU.mult, ALU.add)
                ins.then_inc(w_ready, 1)

            def low_v(c):
                s = c % RING
                if c >= RING:
                    dve.wait_ge(w1_done, NF * (c - RING + 1))
                dve.wait_ge(v_hi_ready, c + 1)
                dve.tensor_tensor(v_lo[:, s, :], p_t2[:, :], v_hi[:, s, :].bitcast(F32), ALU.subtract) \
                   .then_inc(v_lo_ready, 1)

            def gate_ff_out(c):
                if c == NC - 1:
                    return
                s = c % RING
                dve.wait_ge(w2_done, c + 1)
                if c >= RING:
                    dve.wait_ge(y2_ready, c - RING + 1)
                dve.tensor_tensor(steps(gated_ff[:, s, :]), steps(p_y[c % 2][:, :]), over_steps(gate_ff), ALU.mult) \
                   .then_inc(gated_ff_ready, 1)

            def add_b2(c):
                s = c % RING
                if c >= RING:
                    dve.wait_ge(y2_ready, c - RING + 1)
                dve.wait_ge(y1_ready, c + 1)
                dve.tensor_tensor(steps(y1b[:, s, :]), steps(y1[:, c, :]), over_steps(gate_b2), ALU.add) \
                   .then_inc(y1b_ready, 1)

            def last_chunk():
                c = NC - 1
                slot = c % RING
                dve.wait_ge(y1b_ready, NC)
                for k, part in enumerate(LAST_PARTS):
                    at, ff_bank = slice(part.start * D, part.stop * D), p_y[(c + k) % 2]
                    by_step = [128, part.stop - part.start, D]
                    dve.wait_ge(w2_done, NC + k)
                    if k == 0:
                        dve.wait_ge(y2_ready, c - RING + 1)
                    dve.tensor_tensor(gated_ff[:, slot, at].rearrange("p (s d) -> p s d", d=D),
                                      ff_bank[:, at].rearrange("p (s d) -> p s d", d=D),
                                      gate_ff[:, :].unsqueeze(1).to_broadcast(by_step), ALU.mult) \
                       .then_inc(gated_ff_ready, 1)
                    dve.wait_ge(gated_ff_ready, NC + k)
                    dve.tensor_tensor(y2[:, c, at], gated_ff[:, slot, at], y1b[:, slot, at], ALU.add).then_inc(y2_ready, 1)

            def add_ff(c):
                if c == NC - 1:
                    last_chunk()
                    return
                dve.wait_ge(y1b_ready, c + 1)
                dve.wait_ge(gated_ff_ready, c + 1)
                dve.tensor_tensor(y2[:, c, :], gated_ff[:, c % RING, :], y1b[:, c % RING, :], ALU.add).then_inc(y2_ready, 1)

            def raw1(c):
                raw_stats_of(0, c)

            def mean1(c):
                mean_var_of(0, c)

            def raw2(c):
                raw_stats_of(1, c)

            def mean2(c):
                mean_var_of(1, c)

            z0, z1, z2, z3 = (recur(j) for j in range(STEPS))

            dve.wait_ge(mod_b_in_psum, 1)
            link(dve.tensor_copy(gate_a[:, :], p_h[0][:, 0:D]))
            dve.tensor_tensor(gate_d[:, :], gate_a[:, :], p_h[0][:, 2 * D:3 * D], ALU.mult).then_inc(gates_ready, 1)
            copy_bT()
            turn_c(0)
            turn_c(1)
            turn_c(2)
            z0(0)
            turn_c(3)
            z1(0)
            factor_matrices(STEPS, W)
            z2(0)
            dve.wait_ge(chain, count["chain"])
            dve.tensor_tensor(factors[:, STEPS:W, :], factor_part[:, STEPS:W, :], factor_part2[:, STEPS:W, :],
                              ALU.add).then_inc(turns_ready, 1)
            z3(0)
            second_modulation()
            raw1(2)
            gate_state(0)
            add_state(0)
            raw2(0)
            mean2(0)
            mean1(2)
            scale_first_w()
            low_w1(0)
            low_w1(1)
            low_w1(2)
            low_w1(3)
            z0(1)
            z1(1)
            z2(1)
            z3(1)
            raw1(3)
            shift_first_w()
            gate_state(1)
            mean1(3)
            low_v(0)
            add_state(1)
            raw2(1)
            mean2(1)
            z0(2)
            z1(2)
            z2(2)
            z3(2)
            raw1(4)
            mean1(4)
            add_b2(0)
            scale_w(1)
            gate_state(2)
            shift_w(1)
            add_state(2)
            raw2(2)
            low_v(1)
            z0(3)
            mean2(2)
            z1(3)
            z2(3)
            z3(3)
            gate_ff_out(0)
            add_ff(0)
            raw1(5)
            mean1(5)
            scale_w(2)
            gate_state(3)
            shift_w(2)
            add_state(3)
            raw2(3)
            mean2(3)
            low_v(2)
            z0(4)
            z1(4)
            z2(4)
            add_b2(1)
            z3(4)
            gate_ff_out(1)
            raw1(6)
            add_ff(1)
            mean1(6)
            scale_w(3)
            gate_state(4)
            shift_w(3)
            add_state(4)
            raw2(4)
            mean2(4)
            low_v(3)
            z0(5)
            z1(5)
            z2(5)
            add_b2(2)
            z3(5)
            gate_ff_out(2)
            add_ff(2)
            raw1(7)
            mean1(7)
            scale_w(4)
            gate_state(5)
            shift_w(4)
            add_state(5)
            raw2(5)
            mean2(5)
            low_v(4)
            z0(6)
            z1(6)
            z2(6)
            add_b2(3)
            z3(6)
            gate_ff_out(3)
            add_ff(3)
            run([(raw1, 5, 8), (mean1, 5, 8), (scale_w, 2, 5), (gate_state, 3, 6), (shift_w, 2, 5),
                 (add_state, 3, 6), (raw2, 3, 6), (mean2, 3, 6), (low_v, 2, 5), (z0, 4, 7), (add_ff, 0, 4),
                 (z1, 4, 7), (z2, 4, 7), (add_b2, 1, 4), (z3, 4, 7), (gate_ff_out, 1, 4)])

        @block.scalar
        def _(act):
            act.dma_start(cond_sb[:, :], cond).then_inc(cond_landed, 16)
            act.dma_start(wmod[:, 0:2 * D], Wm[:, 0:2 * D]).then_inc(wmod_a_landed, 16)

            def norm(k, c):
                src, dst = (x_sb, n1) if k == 0 else (y1, n2)
                if c >= RING:
                    act.wait_ge([u_part_ready, w_part_ready][k], c - RING + 1)
                act.wait_ge(rstd_ready[k], c + 1)
                for j in range(STEPS):
                    at = slice(j * D, (j + 1) * D)
                    ins = nc.scalar.activation(dst[:, c % RING, at], src[:, c, at], ACT.Identity,
                                               bias=norm_bias[k][:, c, j:j + 1], scale=rstd[k][:, c, j:j + 1])
                ins.then_inc(n_ready[k], 1)

            def copy_uT(c):
                act.wait_ge(u_in_psum, c + 1)
                if c >= RING:
                    act.wait_ge(b_done, c - RING + 1)
                nc.scalar.copy(uT[:, c % RING, :], p_t1[:, :]).then_inc(uT_ready, 1)

            def high_v(c):
                act.wait_ge(w_in_psum, c + 1)
                if c >= RING:
                    act.wait_ge(w1_done, NF * (c - RING + 1))
                nc.scalar.copy(v_hi[:, c % RING, :], p_t2[:, :]).then_inc(v_hi_ready, 1)

            def gelu(f):
                def stage(c):
                    if f == 0 and c == 0:
                        act.wait_ge(b1_col_ready, 1)
                    if f == 0 and c >= 2:
                        act.wait_ge(w2_done, c - 1)
                    act.wait_ge(w1_done, NF * c + f + 1)
                    nc.scalar.activation(h[:, c % 2, f, :], p_h[f % 2][:, :], ACT.Gelu_apprx_tanh,
                                         bias=b1_col[:, f:f + 1]).then_inc(h_ready, 1)
                return stage

            act.wait_ge(ones_ready, 1)
            nc.scalar.activation(first_sine[:, :], ones_row[:, 0:1], ACT.Sin)
            act.wait_ge(condT_in_psum, 1)
            nc.scalar.copy(condT[:, :], p_b[:, 0:NB]).then_inc(condT_ready, 1)
            act.wait_ge(mod_a_in_psum, 1)
            nc.scalar.activation(scale1[:, :], p_y[0][:, D:2 * D], ACT.Identity, bias=1.0)
            nc.scalar.copy(shift1[:, :], p_y[0][:, 0:D]).then_inc(modulation1_ready, 1)
            act.wait_ge(angles_ready, 1)
            nc.scalar.activation(sines[:, :, :], angles[:, :, :], ACT.Sin).then_inc(sines_ready, 1)
            norm(0, 0)
            nc.scalar.activation(first_gelu[:, :], ones_row[:, 0:1], ACT.Gelu_apprx_tanh)
            act.wait_ge(cT_in_psum, 1)
            nc.scalar.copy(cT[:, :, :], p_y[1][:, 0:2 * D].rearrange("p (k d) -> p k d", k=2)).then_inc(cT_ready, 1)
            nc.scalar.copy(b1_col[:, :], p_y[1][:, 2 * D:2 * D + NF]).then_inc(b1_col_ready, 1)
            act.wait_ge(c_im_ready, 1)
            for j in range(STEPS):
                ins = nc.scalar.activation(c_part[:, j, :], p_y[1][:, D:2 * D], ACT.Identity, scale=c_im[:, j:j + 1])
            ins.then_inc(c_part_ready, 1)
            act.wait_ge(w1_landed, 16)
            nc.scalar.copy(w1_hi[:, :], w1_sb[:, :]).then_inc(w1_hi_ready, 1)
            copy_uT(0)
            act.wait_ge(mod_c_in_psum, 1)
            nc.scalar.copy(gate_ff[:, :], p_h[1][:, D:2 * D])
            nc.scalar.activation(scale_ff[:, :], p_h[1][:, 0:D], ACT.Identity, bias=1.0).then_inc(ff_tables_ready, 1)
            norm(0, 1)
            def norm1(c):
                norm(0, c)

            def norm2(c):
                norm(1, c)

            gelu0, gelu1, gelu2, gelu3 = (gelu(f) for f in range(NF))
            copy_uT(1)
            norm1(2)
            high_v(0)
            copy_uT(2)
            gelu0(0)
            norm1(3)
            gelu1(0)
            norm2(1)
            gelu2(0)
            copy_uT(3)
            gelu3(0)
            high_v(1)
            norm1(4)
            gelu0(1)
            gelu1(1)
            run([(gelu3, 0, 1), (norm1, 4, 5), (gelu0, 1, 2), (norm2, 2, 2), (gelu1, 1, 2), (gelu2, 1, 1),
                 (copy_uT, 4, 4), (high_v, 2, 2)])

        @block.tensor
        def _(pe):
            def turn(dst, src, k):
                return pe.transpose(dst, src, ident[0:k, 0:k])

            def modulation(dst, first, width, bias_landed):
                pe.matmul(dst, condT[:, :], wmod[:, first:first + width], start=True, stop=False)
                if first == 0:
                    warm(p_c, 1)
                pe.wait_ge(bias_landed, 16)
                return pe.matmul(dst, ones_row[:, :], mod_bias[:, first:first + width], start=False, stop=True)

            def turn_u(c):
                pe.wait_ge(u_ready, c + 1)
                if c >= 1:
                    pe.wait_ge(uT_ready, c)
                for j in range(STEPS):
                    last = turn(p_t1[:, j * D:(j + 1) * D], u[:, c % RING, j * D:(j + 1) * D], NB)
                last.then_inc(u_in_psum, 1)

            def turn_w(c):
                pe.wait_ge(w_ready, c + 1)
                if c >= 1:
                    pe.wait_ge(v_lo_ready, c)
                for j in range(STEPS):
                    last = turn(p_t2[:, j * D:(j + 1) * D], w[:, c % RING, j * D:(j + 1) * D], NB)
                last.then_inc(w_in_psum, 1)

            halves = [slice(0, R), slice(R, 2 * R)]

            def state_inputs(c):
                pe.wait_ge(uT_ready, c + 1)
                if c == 0:
                    pe.wait_ge(bT_ready, 1)
                else:
                    if c == 1:
                        pe.wait_ge(turns_ready, 2)
                    pe.wait_ge(z_ready, STEPS * c)
                for k, rows in enumerate(halves):
                    last = pe.matmul(p_b[rows, 0:HB], bT[:, 0, :], uT[:, c % RING, k * HB:(k + 1) * HB],
                                     start=True, stop=(c == 0))
                if c >= 1:
                    for rows in halves:
                        pe.matmul(p_b[rows, 0:HB], factors[rows, STEPS, :], z[rows, c - 1, STEPS - 1, :],
                                  start=False, stop=True)
                for j in range(1, STEPS):
                    for k, rows in enumerate(halves):
                        at = j * NB + k * HB
                        last = pe.matmul(p_b[rows, j * HB:(j + 1) * HB], bT[:, j, :], uT[:, c % RING, at:at + HB],
                                         start=True, stop=True)
                last.then_inc(b_done, 1)

            def state_outputs(c):
                pe.wait_ge(z_ready, STEPS * (c + 1))
                if c == 0:
                    pe.wait_ge(c_turned_ready, STEPS)
                else:
                    pe.wait_ge(gated_ready, c)
                for j in range(STEPS):
                    for rows in halves:
                        last = pe.matmul(p_c[rows, j * D:(j + 1) * D], z[rows, c, j, :], c_turned[rows, j, :],
                                         start=True, stop=True)
                last.then_inc(c_done, 1)

            def hidden(f):
                def stage(c):
                    if f == 0:
                        pe.wait_ge(v_hi_ready, c + 1)
                        pe.wait_ge(v_lo_ready, c + 1)
                        if c == 0:
                            pe.wait_ge(w1_split, NF)
                    hi, lo = v_hi[:, c % RING, :], v_lo[:, c % RING, :]
                    if NF * c + f >= 2:
                        pe.wait_ge(h_ready, NF * c + f - 1)
                    elif f == 0:
                        pe.wait_ge(modulation2_ready, 1)
                    tile = slice(f * D, (f + 1) * D)
                    pe.matmul(p_h[f % 2][:, :], w1_lo[:, tile], hi, start=True, stop=False)
                    pe.matmul(p_h[f % 2][:, :], w1_hi[:, tile], lo, start=False, stop=False)
                    pe.matmul(p_h[f % 2][:, :], w1_hi[:, tile], hi, start=False, stop=True).then_inc(w1_done, 1)
                return stage

            def feed_forward(f):
                def stage(c):
                    if f == 0:
                        if c == 0:
                            pe.wait_ge(w2_landed, 16)
                            pe.wait_ge(modulation1_ready, 1)
                        elif c == 1:
                            pe.wait_ge(c_part_ready, 1)
                        else:
                            pe.wait_ge(gated_ff_ready, c - 1)
                    pe.wait_ge(h_ready, NF * c + f + 1)
                    for j in range(STEPS):
                        second = c == NC - 1 and j >= LAST_PARTS[1].start
                        ends = [STEPS - 1] if c < NC - 1 else [part.stop - 1 for part in LAST_PARTS]
                        ff_bank = p_y[1 - c % 2] if second else p_y[c % 2]
                        starts = f == 0 and (j == 0 or second and j == LAST_PARTS[1].start)
                        if starts and second:
                            pe.wait_ge(gated_ff_ready, c)
                        ins = pe.matmul(ff_bank[:, j * D:(j + 1) * D], h[:, c % 2, f, j * NB:(j + 1) * NB],
                                        w2_sb[:, f, :], start=starts, stop=(f == NF - 1 and j in ends))
                        if f == NF - 1 and j in ends:
                            ins.then_inc(w2_done, 1)
                return stage

            def warm(free_bank, times):
                if free_bank is p_y[1]:
                    pe.wait_ge(c_part_ready, 1)
                for _ in range(times):
                    pe.matmul(free_bank[:, 0:D], ident[:, :], ident[:, :], start=True, stop=True)

            pe.wait_ge(ident_ready, 1)
            warm(p_c, 5)
            pe.wait_ge(cond_landed, 16)
            turn(p_b[:, 0:NB], cond_sb[:, :], NB).then_inc(condT_in_psum, 1)
            warm(p_c, 3)
            pe.wait_ge(condT_ready, 1)
            pe.wait_ge(wmod_a_landed, 16)
            pe.wait_ge(ones_ready, 1)
            modulation(p_y[0][:, 0:2 * D], 0, 2 * D, bm_landed).then_inc(mod_a_in_psum, 1)
            pe.wait_ge(wmod_landed, 16)
            modulation(p_h[0][:, 0:2 * D], 2 * D, 2 * D, bm_landed)
            pe.wait_ge(free_rows_landed, 32)
            pe.matmul(p_h[0][:, 2 * D:4 * D], ones_row[:, :], free_rows[:, :], start=True, stop=True) \
              .then_inc(mod_b_in_psum, 1)
            pe.wait_ge(wc_landed, 16)
            modulation(p_h[1][:, :], 4 * D, 4 * D, bc_landed).then_inc(mod_c_in_psum, 1)
            pe.wait_ge(c_landed, 32)
            turn(p_y[1][:, 0:D], c_parts[:, 0:4, :].rearrange("d g p -> d (g p)"), D)
            turn(p_y[1][:, D:2 * D], c_parts[:, 1:5, :].rearrange("d g p -> d (g p)"), D)
            pe.wait_ge(b1_landed, 16)
            turn(p_y[1][:, 2 * D:2 * D + NF], b1_rows[:, :], NF).then_inc(cT_in_psum, 1)
            warm(p_c, 9)
            turn_u(0)
            warm(p_c, 1)
            pe.wait_ge(b_landed, 32)
            pe.wait_ge(turns_ready, 1)
            pe.matmul(p_t2[:, 0:STEPS * R], b_parts[:, :], factors[0:R, 0:STEPS, :].rearrange("p s r -> p (s r)"),
                      start=True, stop=True).then_inc(bT_in_psum, 1)
            state_inputs(0)
            warm(p_y[1], 5)
            state_outputs(0)

            hidden0, hidden1, hidden2, hidden3 = (hidden(f) for f in range(NF))
            ff0, ff1, ff2, ff3 = (feed_forward(f) for f in range(NF))
            warm(p_y[1], 4)
            turn_u(1)
            warm(p_y[1], 2)
            state_inputs(1)
            warm(p_y[1], 12)
            state_outputs(1)
            warm(p_y[1], 2)
            turn_w(0)
            warm(p_y[1], 5)
            turn_u(2)
            hidden0(0)
            hidden1(0)
            state_inputs(2)
            ff0(0)
            hidden2(0)
            state_outputs(2)
            hidden3(0)
            ff1(0)
            turn_u(3)
            ff2(0)
            turn_w(1)
            state_inputs(3)
            ff3(0)
            hidden0(1)
            hidden1(1)
            state_outputs(3)
            hidden2(1)
            ff0(1)
            ff1(1)
            turn_u(4)
            hidden3(1)
            turn_w(2)
            ff2(1)
            state_inputs(4)
            ff3(1)
            hidden0(2)
            hidden1(2)
            state_outputs(4)
            hidden2(2)
            ff0(2)
            ff1(2)
            turn_u(5)
            turn_w(3)
            hidden3(2)
            ff2(2)
            state_inputs(5)
            ff3(2)
            hidden0(3)
            hidden1(3)
            state_outputs(5)
            hidden2(3)
            ff0(3)
            ff1(3)
            ff2(3)
            turn_u(6)
            turn_w(4)
            hidden3(3)
            state_inputs(6)
            ff3(3)
            run([(hidden1, 0, 4), (state_outputs, 2, 6), (hidden2, 0, 4), (ff0, 0, 4), (ff1, 0, 4),
                 (turn_u, 3, 7), (turn_w, 1, 5), (hidden3, 0, 4), (ff2, 0, 4), (state_inputs, 3, 7),
                 (hidden0, 1, 4), (ff3, 0, 4)])


_INS = ['x', 'cond_1024', 'L0_cond_Wm', 'L0_cond_bm', 'L0_cond_Lam_re', 'L0_cond_Lam_im', 'L0_cond_B_re',
        'L0_cond_B_im', 'L0_cond_C_re', 'L0_cond_C_im', 'L0_cond_D_diag', 'L0_cond_log_step', 'L0_cond_Wc',
        'L0_cond_bc', 'L0_cond_W1', 'L0_cond_b1', 'L0_cond_W2', 'L0_cond_b2']
_OUTS = [((128, 32, 128), 'float32')]


def kernel(**inputs):
    import numpy as _np
    import concourse.bacc as _bacc
    from concourse import mybir as _mybir
    from concourse.bass_utils import run_bass_kernel_spmd as _run

    nc = _bacc.Bacc("TRN2", target_bir_lowering=False, num_devices=1)
    arrays, args = {}, []
    for name in _INS:
        a = _np.ascontiguousarray(inputs[name])
        arrays[f"in_{name}_dram"] = a
        args.append(nc.dram_tensor(f"in_{name}_dram", a.shape, _mybir.dt.from_np(a.dtype), kind="ExternalInput").ap())
    for i, (shape, dtype) in enumerate(_OUTS):
        dt = _mybir.dt.from_np(_np.dtype(dtype))
        args.append(nc.dram_tensor(f"out_{i}_dram", shape, dt, kind="ExternalOutput").ap())
    conditioned_s5_block(nc, *args)
    r = _run(nc, [arrays], core_ids=[0])
    return r.results[0]["out_0_dram"]
```
